# Optimizing a Trainium2 kernel written in Bass

```python
import numpy as np
import jax
import jax.numpy as jnp

def _softmax(x, axis=-1):
    return jax.nn.softmax(x, axis=axis)

def _gelu(x):
    return jax.nn.gelu(x, approximate=True)

def _silu(x):
    return jax.nn.silu(x)

def _sigmoid(x):
    return jax.nn.sigmoid(x)

def _layernorm(x, axis=-1, eps=1e-05):
    m = jnp.mean(x, axis=axis, keepdims=True)
    v = jnp.var(x, axis=axis, keepdims=True)
    return (x - m) / jnp.sqrt(v + eps)

def _scatter_add(tgt, idx, src, axis=0):
    return tgt.at[idx].add(src)

def _segment_sum(src, seg, n):
    return jax.ops.segment_sum(src, seg, n)
kernel_name = 'mk_sandwich_d1_jaxref_r8_2447eb'

def setup_inputs(seed: int=0):
    np.random.seed(seed)
    _w = jnp.asarray

    def _L0_attn_setup():
        import jax, jax.numpy as jnp
        import numpy as np
        EMBED_DIM = 256
        N_HEADS = 16
        HEAD_DIM = EMBED_DIM // N_HEADS
        B, T = (2, 256)

        def rope(x, pos):
            half = HEAD_DIM // 2
            freqs = 10000.0 ** (-jnp.arange(half, dtype=jnp.float32) / half)
            theta = pos[:, None].astype(jnp.float32) * freqs[None, :]
            sin = jnp.sin(theta)[None, None, :, :]
            cos = jnp.cos(theta)[None, None, :, :]
            x1 = x[..., 0::2]
            x2 = x[..., 1::2]
            return jnp.concatenate([x1 * cos - x2 * sin, x1 * sin + x2 * cos], axis=-1)
        key = jax.random.key(seed)
        k1, k2, k3, k4, k5 = jax.random.split(key, 5)
        bound_qkv = 1.0 / np.sqrt(EMBED_DIM)
        return {'x': jax.random.normal(k1, (B, T, EMBED_DIM), dtype=jnp.float32), 'w_qkv': jax.random.uniform(k2, (3 * EMBED_DIM, EMBED_DIM), minval=-bound_qkv, maxval=bound_qkv), 'b_qkv': jax.random.uniform(k3, (3 * EMBED_DIM,), minval=-bound_qkv, maxval=bound_qkv), 'w_out': jax.random.uniform(k4, (EMBED_DIM, EMBED_DIM), minval=-bound_qkv, maxval=bound_qkv), 'b_out': jax.random.uniform(k5, (EMBED_DIM,), minval=-bound_qkv, maxval=bound_qkv)}
    _L0_attn_in = _L0_attn_setup()

    def _L0_ffn_setup():
        import jax, jax.numpy as jnp
        import numpy as np
        B, S, D, H = (4, 256, 256, 1024)

        def fwht(x):
            orig_shape = x.shape
            n = orig_shape[-1]
            x = x.reshape(-1, n)
            h = 1
            while h < n:
                xb = x.reshape(-1, n // (2 * h), 2, h)
                a = xb[:, :, 0, :]
                b = xb[:, :, 1, :]
                x = jnp.stack([a + b, a - b], axis=2).reshape(-1, n)
                h *= 2
            scale = jnp.asarray(1.0 / np.sqrt(n), dtype=x.dtype)
            return (x * scale).reshape(orig_shape)
        key = jax.random.key(seed)
        kx, k1, k2, k3 = jax.random.split(key, 4)
        x = jax.random.normal(kx, (B, S, D), dtype=jnp.float32)
        W1 = jax.random.normal(k1, (H, D), dtype=jnp.float32) * (1.0 / np.sqrt(D))
        W2 = jax.random.normal(k2, (D, H), dtype=jnp.float32) * (1.0 / np.sqrt(H))
        W3 = jax.random.normal(k3, (H, D), dtype=jnp.float32) * (1.0 / np.sqrt(D))
        return {'x': x, 'W1': W1, 'W2': W2, 'W3': W3}
    _L0_ffn_in = _L0_ffn_setup()
    _d = {'L0_attn_x': _L0_attn_in['x'], 'L0_attn_w_qkv': _L0_attn_in['w_qkv'], 'L0_attn_b_qkv': _L0_attn_in['b_qkv'], 'L0_attn_w_out': _L0_attn_in['w_out'], 'L0_attn_b_out': _L0_attn_in['b_out'], 'L0_ffn_W1': _L0_ffn_in['W1'], 'L0_ffn_W2': _L0_ffn_in['W2'], 'L0_ffn_W3': _L0_ffn_in['W3']}
    _x0 = _d['L0_attn_x']
    _d['L0_attn_x'] = jax.random.normal(jax.random.fold_in(jax.random.key(seed), 1), (4, 512, 256), dtype=_x0.dtype)
    del _x0
    return _d

def reference(L0_attn_x, L0_attn_w_qkv, L0_attn_b_qkv, L0_attn_w_out, L0_attn_b_out, L0_ffn_W1, L0_ffn_W2, L0_ffn_W3):

    def _L0_attn_ref(x, w_qkv, b_qkv, w_out, b_out):
        import jax, jax.numpy as jnp
        import numpy as np
        EMBED_DIM = 256
        N_HEADS = 16
        HEAD_DIM = EMBED_DIM // N_HEADS
        B, T = (2, 256)

        def rope(x, pos):
            half = HEAD_DIM // 2
            freqs = 10000.0 ** (-jnp.arange(half, dtype=jnp.float32) / half)
            theta = pos[:, None].astype(jnp.float32) * freqs[None, :]
            sin = jnp.sin(theta)[None, None, :, :]
            cos = jnp.cos(theta)[None, None, :, :]
            x1 = x[..., 0::2]
            x2 = x[..., 1::2]
            return jnp.concatenate([x1 * cos - x2 * sin, x1 * sin + x2 * cos], axis=-1)
        Bn, Tn, D = x.shape
        qkv = x @ w_qkv.T + b_qkv
        q, k, v = jnp.split(qkv, 3, axis=-1)

        def reshape(t):
            return t.reshape(Bn, Tn, N_HEADS, HEAD_DIM).transpose(0, 2, 1, 3)
        q, k, v = map(reshape, (q, k, v))
        pos = jnp.arange(Tn)
        q = rope(q, pos)
        k = rope(k, pos)
        scale = HEAD_DIM ** (-0.5)
        attn = jnp.einsum('bhqd,bhkd->bhqk', q, k) * scale
        causal = jnp.triu(jnp.ones((Tn, Tn), dtype=bool), k=1)
        attn = jnp.where(causal[None, None], -jnp.inf, attn)
        attn = jax.nn.softmax(attn, axis=-1)
        out = jnp.einsum('bhqk,bhkd->bhqd', attn, v)
        out = out.transpose(0, 2, 1, 3).reshape(Bn, Tn, D)
        return out @ w_out.T + b_out

    def _L0_ffn_ref(x, W1, W2, W3):
        import jax, jax.numpy as jnp
        import numpy as np
        B, S, D, H = (4, 256, 256, 1024)

        def fwht(x):
            orig_shape = x.shape
            n = orig_shape[-1]
            x = x.reshape(-1, n)
            h = 1
            while h < n:
                xb = x.reshape(-1, n // (2 * h), 2, h)
                a = xb[:, :, 0, :]
                b = xb[:, :, 1, :]
                x = jnp.stack([a + b, a - b], axis=2).reshape(-1, n)
                h *= 2
            scale = jnp.asarray(1.0 / np.sqrt(n), dtype=x.dtype)
            return (x * scale).reshape(orig_shape)
        up_gate = jnp.einsum('bsd,hd->bsh', x, W1)
        up_lin = jnp.einsum('bsd,hd->bsh', x, W3)
        hidden = jax.nn.silu(up_gate) * up_lin
        hidden = fwht(hidden)
        out = jnp.einsum('bsh,dh->bsd', hidden, W2)
        return out
    x = L0_attn_x
    x = x + _layernorm(_L0_attn_ref(_layernorm(x, axis=-1), L0_attn_w_qkv, L0_attn_b_qkv, L0_attn_w_out, L0_attn_b_out), axis=-1)
    x = x + _layernorm(_L0_ffn_ref(_layernorm(x, axis=-1), L0_ffn_W1, L0_ffn_W2, L0_ffn_W3), axis=-1)
    return x

_drawn_inputs = setup_inputs


def setup_inputs(seed=0):
    import zlib

    import numpy as np

    out = dict(_drawn_inputs(seed))
    spreads = {}
    factors = {}
    for name, (base, spread) in spreads.items():
        noise = np.random.default_rng([zlib.crc32(name.encode()), seed]).standard_normal(out[name].shape)
        drawn = base * np.exp(spread * noise) if base else spread * noise
        out[name] = jnp.asarray(drawn.astype(out[name].dtype))
    for name, factor in factors.items():
        out[name] = (out[name] * factor).astype(out[name].dtype)
    return out
```

```python
from contextlib import ExitStack

import concourse.bass as bass
from concourse import mybir

F32 = mybir.dt.float32
F32R = mybir.dt.float32r
BF16 = mybir.dt.bfloat16
I32 = mybir.dt.int32
ALU = mybir.AluOpType
ACT = mybir.ActivationFunctionType
AX = mybir.AxisListType

BATCHES, TOKENS, DIM, HIDDEN, HEADS = 4, 512, 256, 1024, 16
HEAD = DIM // HEADS
P = 128
TILES = TOKENS // P
CH = DIM // P
HCH = HIDDEN // P
PAIRS = HEADS // 2
GROUPS = HEADS // 4
HALF = HEAD // 2
EPS = 1e-5
SCALE = HEAD ** -0.5
W2_SCALE = 0.5 * HIDDEN ** -0.5
QK_ROWS = 3 * 2 * HEAD
MAX_ROWS = 2 * HEADS
KEY_COL = [0, 512, 1024, 896]
P_COLS = 1280
UNITS = []
for _qt in range(TILES):
    _n = TILES // (_qt + 1)
    _n = 1 if _n < 1 else _n
    UNITS += [("scores", _qt, list(range(h, h + _n))) for h in range(0, HEADS, _n)]
for _qt in range(TILES):
    _last = max(i for i, u in enumerate(UNITS) if u[0] == "scores" and u[1] == _qt)
    UNITS.insert(min(_last + 4, len(UNITS)), ("turn", _qt, []))
N_UNITS = len(UNITS)
LAG = 1
UNITS_AT = [0, 0, 0, 6, 8, 8, 8, 9, N_UNITS - 39]
SPLIT_AT = [sum(UNITS_AT[:i]) for i in range(len(UNITS_AT) + 1)]
NEWTON = 3
LN_STEPS = TILES + 8 + 3 * NEWTON + 1


def layer_kernel(nc, x, w_qkv, b_qkv, w_out, b_out, w1, w3, w2, rope, hadamard, eye, mask, selector, out):
    ctx = ExitStack()
    with ctx:
        def sb(name, shape, dt=F32):
            return ctx.enter_context(nc.sbuf_tensor(name, shape, dt))

        def sem(name):
            return ctx.enter_context(nc.semaphore(name))

        wqkv_s = sb("wqkv_s", [P, 2, CH, 3 * DIM], F32R)
        wo_s = sb("wo_s", [P, 2, CH, DIM], F32R)
        w1_s = sb("w1_s", [P, 2, CH, HIDDEN], F32R)
        w3_s = sb("w3_s", [P, 2, CH, HIDDEN], F32R)
        w2_s = sb("w2_s", [P, 2, HCH, DIM], F32R)
        bqkv = sb("bqkv", [P, 3 * DIM])
        bout = sb("bout", [P, DIM])
        rope_t = sb("rope_t", [P, TILES, 2, 2 * HALF])
        had = sb("had", [P, P])
        ident = sb("ident", [P, P])
        ident_r = sb("ident_r", [P, P], F32R)
        ident_b = sb("ident_b", [P, P], BF16)
        mask_f = sb("mask_f", [P, P])
        mask_b = sb("mask_b", [P, P], BF16)
        sel = sb("sel", [P, HEADS])
        q_t = sb("q_t", [P, PAIRS, TOKENS], F32R)
        k_t = sb("k_t", [P, HEADS, TOKENS], F32R)
        xt = q_t[:, 0:4, :].rearrange("p (s c) t -> p s c t", s=2)
        v_t = sb("v_t", [P, TILES, HEADS, 2 * HEAD])
        max_row = sb("max_row", [P, TOKENS], F32R)
        def arena(name, words):
            start = nc.sbuf_base
            sb(name, [P, words])

            def place(tensor, shape, dt=F32, word=0):
                words_used = 1
                for n in shape[1:]:
                    words_used *= n
                assert word + words_used <= words
                return nc.alloc_sbuf_tensor_at(tensor, shape, dt, offset=start + 4 * word)
            return place

        place = arena("attend_arena", 8 * P_COLS)
        probs = place("probs", [P, 8, P_COLS])
        qk_s = place("qk_s", [P, 2, 4, TOKENS], F32R)
        qk_b = place("qk_b", [P, 2, 512], word=4096)
        rot = place("rot", [P, 2, 512], word=5120)
        rot_s = place("rot_s", [P, 512], word=6144)[:, :]
        gate = place("gate", [P, 2, TOKENS], word=6656)
        hid_s = place("hid_s", [P, 2, 2, TOKENS], F32R, word=7680)
        raw_wqkv = place("raw_wqkv", [P, CH * 3 * DIM], word=6656)[:, :]
        raw_wo = place("raw_wo", [P, CH * DIM], word=8192)[:, :]
        stage_a = place("butterfly_b", [P, HCH * DIM], word=6656)[:, :]
        place = arena("turned_arena", 2 * CH * TOKENS)
        xt2 = place("xt2", [P, 2, CH, TOKENS], F32R)
        raw_w1 = place("raw_w1", [P, CH * HIDDEN])[:, :]
        o_t = sb("o_t", [P, GROUPS, TOKENS])
        xa = sb("xa", [P, TILES, DIM])
        xy = sb("xy", [P, 2, TILES, DIM])
        xr, y = xy[:, 0, :, :], xy[:, 1, :, :]
        raw_w2 = o_t[:, :, :].rearrange("p a b -> p (a b)")
        raw_w3 = xy[:, :, :, :].rearrange("p a b c -> p (a b c)")
        maxima = sb("maxima", [P, HEADS])
        max_s = sb("max_s", [P, 2, HEADS], F32R)
        recip = sb("recip", [P, 2, HEADS])
        stats = sb("stats", [P, TILES, 6])
        nw = sb("nw", [P, 6, TILES])
        rstd = {n: sb("rstd_" + n, [P, TILES]) for n in ("x", "y", "h", "z")}
        shift = {n: sb("shift_" + n, [P, TILES]) for n in ("x", "y", "h", "z")}
        scratch = nc.dram_tensor("qk_scratch", [2, 2 * DIM, TOKENS], F32, kind="Internal").ap()
        q_words, k_words = q_t[:, :, :].bitcast(F32), k_t[:, :, :].bitcast(F32)

        ps = ctx.enter_context(nc.psum_tensor("ps", [P, 8, 512], F32))

        names = """w_qkv_in w_in const_in x_in xr_in scratch_in qk_in maxrow_in out_sent
            split_h split_l made_sel zeroed ident_made had_done had_copy butterfly ones_made
            ln_x ln_y ln_h ln_z norm_x turned_x xt_h xt_l qkv_done qk_biased v_biased roped_c roped_s rotated
            turned_qk qk_h qk_l cutting scored maxed max_h max_l
            st_done exp_done masked pv_done o_copied
            turned_o recips normed turned_n on_h on_l y_done y_biased norm_y resid norm_h turned_h xt2_h xt2_l
            up_done tanh_done gated hidden hid_h hid_l down_done norm_z final""".split()
        S = {n: sem("s_" + n) for n in names}
        block = ctx.enter_context(nc.Block())

        def bank(n, cols=512):
            return ps[:, n, 0:cols]

        def triple(eng, o, lhs, rhs, first, last, skip=False):
            for n, (i, j) in enumerate(((0, 0), (0, 1), (1, 0))):
                ins = eng.matmul(o, lhs(i), rhs(j), start=first and n == 0, stop=last and n == 2,
                                 skip_group_check=skip)
            return ins

        @block.sync
        def _(sp):
            def load_x(b):
                xv = x[bass.ds(b * TOKENS, TOKENS), :].rearrange("(t p) d -> p t d", p=P)
                sp.dma_start(xa[:, :, :], xv).then_inc(S["x_in"], 16)

            def load_xr(b):
                xv = x[bass.ds(b * TOKENS, TOKENS), :].rearrange("(t p) d -> p t d", p=P)
                sp.dma_start(xr, xv).then_inc(S["xr_in"], 16)

            def pack_qk(b):
                for s, done in ((0, "qk_h"), (1, "qk_l")):
                    sp.wait_ge(S[done], b * TILES + TILES)
                    sp.dma_start(scratch[s].rearrange("(c p) t -> p c t", p=P), qk_s[:, s, :, :].bitcast(F32))\
                      .then_inc(S["scratch_in"], 16)
                sp.wait_ge(S["scratch_in"], b * 32 + 32)
                for j, (qs, ks) in enumerate(((0, 0), (0, 1), (1, 0))):
                    sp.dma_start(q_words[32 * j:32 * j + 32, :, :],
                                 scratch[qs, 0:DIM, :].rearrange("(a p) t -> p a t", p=32))\
                      .then_inc(S["qk_in"], 16)
                    kp = scratch[ks, DIM:2 * DIM, :].rearrange("(a e p) t -> e p a t", e=2, p=HEAD)
                    for e in range(2):
                        dst = k_words[32 * j + HEAD * e:32 * j + HEAD * e + HEAD, :, :]
                        sp.dma_start(dst.rearrange("p (a e) t -> p e a t", e=2)[:, e, :, :], kp[e])\
                          .then_inc(S["qk_in"], 16)

            def fill_max_rows(b):
                sp.wait_ge(S["maxed"], (b + 1) * N_UNITS)
                for a in range(PAIRS):
                    sp.dma_start(q_words[QK_ROWS:P, a, :], max_row[QK_ROWS:P, :].bitcast(F32)).then_inc(S["maxrow_in"], 16)

            def store(b):
                sp.wait_ge(S["final"], b * TILES + TILES)
                ov = out[bass.ds(b * TOKENS, TOKENS), :].rearrange("(t p) d -> p t d", p=P)
                sp.dma_start(ov, y).then_inc(S["out_sent"], 16)

            load_x(0)
            sp.dma_start(raw_wqkv.rearrange("p (c n) -> p c n", c=CH),
                         w_qkv.rearrange("(c p) n -> p c n", p=P)).then_inc(S["w_qkv_in"], 16)
            sp.dma_start(ident[:, :], eye).then_inc(S["const_in"], 16)
            sp.dma_start(rope_t[:, :, :, :].rearrange("p t a b -> p t (a b)"),
                         rope.rearrange("(t p) a -> p t a", p=P)).then_inc(S["const_in"], 16)
            sp.dma_start(bqkv[:, :], b_qkv.partition_broadcast(P)).then_inc(S["const_in"], 16)
            sp.dma_start(bout[:, :], b_out.partition_broadcast(P)).then_inc(S["const_in"], 16)
            sp.dma_start(mask_f[:, :], mask).then_inc(S["const_in"], 16)
            sp.dma_start(sel[QK_ROWS:P, :], selector).then_inc(S["const_in"], 16)
            sp.dma_start(had[:, :], hadamard).then_inc(S["const_in"], 16)
            sp.dma_start(raw_w2.rearrange("p (c n) -> p c n", c=HCH),
                         w2.rearrange("(c p) n -> p c n", p=P)).then_inc(S["w_in"], 16)
            sp.dma_start(raw_wo.rearrange("p (c n) -> p c n", c=CH),
                         w_out.rearrange("(c p) n -> p c n", p=P)).then_inc(S["w_in"], 16)
            sp.dma_start(raw_w1.rearrange("p (c n) -> p c n", c=CH),
                         w1.rearrange("(c p) n -> p c n", p=P)).then_inc(S["w_in"], 16)
            sp.dma_start(raw_w3.rearrange("p (c n) -> p c n", c=CH),
                         w3.rearrange("(c p) n -> p c n", p=P)).then_inc(S["w_in"], 16)
            sp.wait_ge(S["zeroed"], 2)
            pack_qk(0)
            fill_max_rows(0)
            sp.wait_ge(S["split_l"], 4)
            load_xr(0)
            with sp.Fori(0, BATCHES - 1) as b:
                sp.wait_ge(S["turned_x"], b * TILES + TILES)
                load_x(b + 1)
                pack_qk(b + 1)
                fill_max_rows(b + 1)
                store(b)
                sp.wait_ge(S["out_sent"], b * 16 + 16)
                load_xr(b + 1)
            store(BATCHES - 1)
            sp.wait_ge(S["out_sent"], 16 * BATCHES)

        @block.tensor
        def _(pe):
            def turn_x(b):
                for t in range(TILES):
                    pe.wait_ge(S["norm_x"], b * TILES + t + 1)
                    if t >= 2:
                        pe.wait_ge(S["xt_l"], b * TILES + t - 1)
                    for c in range(CH):
                        ins = pe.transpose(ps[:, t % 2, c * P:c * P + P], xa[:, t, c * P:c * P + P], ident[:, :])
                    ins.then_inc(S["turned_x"], 1)

            def qkv(b):
                for t in range(TILES):
                    pe.wait_ge(S["xt_l"], b * TILES + max(t + 1, 2 * (t == 0) or t + 1))
                    if t == 0:
                        pe.wait_ge(S["xt_l"], b * TILES + TILES)
                    if t >= 2:
                        pe.wait_ge(S["v_biased"], b * TILES + t - 1)
                    lhs = lambda c: (lambda s: xt[:, s, c, t * P:t * P + P])
                    for c in range(CH):
                        triple(pe, ps[:, t % 2, :], lhs(c), lambda s: wqkv_s[:, s, c, 0:2 * DIM], c == 0, c == CH - 1)
                    for c in range(CH):
                        ins = triple(pe, ps[:, 2 + t % 2, 0:DIM], lhs(c), lambda s: wqkv_s[:, s, c, 2 * DIM:3 * DIM],
                                     c == 0, c == CH - 1)
                    ins.then_inc(S["qkv_done"], 1)

            def turn_qk(b, t):
                pe.wait_ge(S["rotated"], b * TILES + t + 1)
                if t >= 2:
                    pe.wait_ge(S["qk_l"], b * TILES + t - 1)
                for c in range(4):
                    ins = pe.transpose(ps[:, 6 + t % 2, c * P:c * P + P], rot[:, t % 2, c * P:c * P + P], ident[:, :])
                ins.then_inc(S["turned_qk"], 1)

            def score_unit(b, n):
                kind, qt, heads = UNITS[n]
                if n == 0:
                    pe.wait_ge(S["qk_in"], (b + 1) * 144)
                    pe.wait_ge(S["qk_l"], b * TILES + TILES)
                if n >= 2:
                    pe.wait_ge(S["maxed"], b * N_UNITS + n - 1)
                o = ps[:, 6 + n % 2, :]
                if kind == "turn":
                    pe.wait_ge(S["max_l"], b * TILES + qt + 1)
                    pe.transpose(o[0:MAX_ROWS, 0:P].bitcast(F32R), max_s[:, :, :].rearrange("p s h -> p (s h)"),
                                 ident_r[:, :]).then_inc(S["scored"], 1)
                    return
                keys = (qt + 1) * P
                for i, h in enumerate(heads):
                    pe.matmul(o[:, i * keys:(i + 1) * keys], q_t[0:QK_ROWS, h // 2, qt * P:qt * P + P],
                              k_t[0:QK_ROWS, h, 0:keys], start=(i == 0), stop=False, skip_group_check=True)
                    ins = pe.matmul(o[:, (i + 1) * keys - P:(i + 1) * keys], ident_b[:, :], mask_b[:, :],
                                    start=False, stop=(i == len(heads) - 1), skip_group_check=True)
                ins.then_inc(S["scored"], 1)

            def score_t(b, h):
                if h >= 2:
                    pe.wait_ge(S["exp_done"], b * HEADS + h - 1)
                if h == 1:
                    pe.wait_ge(S["norm_z"], b * TILES + TILES)
                for kt in range(TILES):
                    col = 3 * (h % 2) * 512 + KEY_COL[kt]
                    n = TOKENS - kt * P
                    ins = pe.matmul(ps[:, col // 512, col % 512:col % 512 + n], k_t[:, h, kt * P:kt * P + P],
                                    q_t[:, h // 2, kt * P:TOKENS], start=(kt != 3), stop=(kt != 1), skip_group_check=True)
                ins.then_inc(S["st_done"], 1)

            def values(b, g, kt):
                if kt == 0:
                    pe.wait_ge(S["masked"], b * GROUPS + g + 1)
                    if g >= 2:
                        pe.wait_ge(S["o_copied"], b * GROUPS + g - 1)
                for j in range(4):
                    h = 4 * g + j
                    ins = pe.matmul(ps[32 * j:32 * j + 32, 6 + g % 2, kt * P:TOKENS], v_t[:, kt, h, :],
                                    probs[:, 4 * (g % 2) + j, KEY_COL[kt]:KEY_COL[kt] + TOKENS - kt * P],
                                    start=(kt == 0), stop=(kt == TILES - 1), skip_group_check=True)
                if kt == TILES - 1:
                    ins.then_inc(S["pv_done"], 1)

            def attend(b):
                pe.wait_ge(S["maxrow_in"], (b + 1) * 16 * PAIRS)
                pe.wait_ge(S["maxed"], (b + 1) * N_UNITS)
                for h in range(4):
                    score_t(b, h)
                for g in range(GROUPS):
                    for j in range(4):
                        if g < GROUPS - 1:
                            score_t(b, 4 * (g + 1) + j)
                        values(b, g, j)

            def project(b):
                for t in range(TILES + 2):
                    if t < TILES:
                        if t == 0:
                            pe.wait_ge(S["o_copied"], b * GROUPS + GROUPS)
                        if t >= 2:
                            pe.wait_ge(S["normed"], b * TILES + t - 1)
                        for g in range(GROUPS):
                            ins = pe.transpose(ps[:, 2 + t % 2, g * P:g * P + P], o_t[:, g, t * P:t * P + P], ident[:, :])
                        ins.then_inc(S["turned_o"], 1)
                    if 1 <= t <= TILES:
                        n = t - 1
                        pe.wait_ge(S["normed"], b * TILES + n + 1)
                        if n >= 2:
                            pe.wait_ge(S["on_l"], b * TILES + n - 1)
                        for c in range(CH):
                            ins = pe.transpose(ps[:, 4 + n % 2, c * P:c * P + P], y[:, n, c * P:c * P + P], ident[:, :])
                        ins.then_inc(S["turned_n"], 1)
                    if t >= 2:
                        n = t - 2
                        pe.wait_ge(S["on_l"], b * TILES + n + 1)
                        if n >= 2:
                            pe.wait_ge(S["y_biased"], b * TILES + n - 1)
                        for c in range(CH):
                            ins = triple(pe, ps[:, 6 + n % 2, 0:DIM], lambda s: xt2[:, s, c, n * P:n * P + P],
                                         lambda s: wo_s[:, s, c, :], c == 0, c == CH - 1)
                        ins.then_inc(S["y_done"], 1)

            def turn_h(b):
                for t in range(TILES):
                    pe.wait_ge(S["norm_h"], b * TILES + t + 1)
                    if t >= 2:
                        pe.wait_ge(S["xt2_l"], b * TILES + t - 1)
                    for c in range(CH):
                        ins = pe.transpose(ps[:, 4 + t % 2, c * P:c * P + P], y[:, t, c * P:c * P + P], ident[:, :])
                    ins.then_inc(S["turned_h"], 1)

            def up(b, a):
                if a == 0:
                    pe.wait_ge(S["xt2_l"], b * TILES + TILES)
                else:
                    if a >= 2:
                        pe.wait_ge(S["hidden"], b * HCH + a - 1)
                for n, w in enumerate((w1_s, w3_s)):
                    for c in range(CH):
                        ins = triple(pe, ps[:, 2 * (a % 2) + n, :], lambda s: w[:, s, c, a * P:a * P + P],
                                     lambda s: xt2[:, s, c, :], c == 0, c == CH - 1)
                ins.then_inc(S["up_done"], 1)

            def down(b, a):
                pe.wait_ge(S["hid_l"], b * HCH + a + 1)
                for t in range(TILES):
                    ins = triple(pe, ps[:, 4 + t // 2, (t % 2) * DIM:(t % 2) * DIM + DIM],
                                 lambda s: hid_s[:, a % 2, s, t * P:t * P + P], lambda s: w2_s[:, s, a, :],
                                 a == 0 and t % 2 == 0, a == HCH - 1 and t % 2 == 1, skip=True)
                ins.then_inc(S["down_done"], 1)

            def feed_forward(b, ahead):
                for a in range(HCH + LAG):
                    if a < HCH:
                        up(b, a)
                    if ahead and a < TILES:
                        turn_qk(b + 1, a)
                    if a >= LAG:
                        down(b, a - LAG)
                    if ahead:
                        for n in range(SPLIT_AT[a], SPLIT_AT[a + 1]):
                            score_unit(b + 1, n)

            pe.wait_ge(S["const_in"], 16 * 7)
            turn_x(0)
            pe.wait_ge(S["split_l"], 1)
            qkv(0)
            for t in range(TILES):
                turn_qk(0, t)
            pe.wait_ge(S["w_in"], 64)
            for n in range(4):
                ins = pe.matmul(bank(n), had[:, :], raw_w2[:, n * 512:n * 512 + 512], start=True, stop=True)
            ins.then_inc(S["had_done"], 1)
            pe.wait_ge(S["ident_made"], 2)
            for n in range(N_UNITS):
                score_unit(0, n)
            pe.wait_ge(S["made_sel"], 1)
            pe.wait_ge(S["had_copy"], 1)
            pe.wait_ge(S["ones_made"], 1)
            pe.wait_ge(S["split_l"], 5)
            with pe.Fori(0, BATCHES - 1) as b:
                attend(b)
                turn_x(b + 1)
                project(b)
                qkv(b + 1)
                turn_h(b)
                feed_forward(b, True)
            attend(BATCHES - 1)
            project(BATCHES - 1)
            turn_h(BATCHES - 1)
            feed_forward(BATCHES - 1, False)

        @block.scalar
        def _(act):
            def normalize(b, which, src, dst, done):
                act.wait_ge(S["ln_" + which], (b + 1) * LN_STEPS)
                for t in range(TILES):
                    act.activation(dst[:, t, :], src(t), ACT.Identity, bias=shift[which][:, t:t + 1],
                                   scale=rstd[which][:, t:t + 1]).then_inc(S[done], 1)

            def high(b, t, turned, src, dst, done):
                act.wait_ge(S[turned], b * TILES + t + 1)
                act.activation(dst, src, ACT.Copy).then_inc(S[done], 1)

            def xt_high(b):
                for t in range(TILES):
                    high(b, t, "turned_x", ps[:, t % 2, 0:DIM].rearrange("p (c n) -> p c n", c=CH),
                         xt[:, 0, :, t * P:t * P + P], "xt_h")

            def qk_high(b, t):
                high(b, t, "turned_qk", ps[:, 6 + t % 2, :].rearrange("p (c n) -> p c n", c=4),
                     qk_s[:, 0, :, t * P:t * P + P], "qk_h")

            def exps(b, h):
                if h >= 8:
                    act.wait_ge(S["pv_done"], b * GROUPS + h // 4 - 1)
                act.wait_ge(S["st_done"], b * HEADS + h + 1)
                src = ps[:, 3 * (h % 2):3 * (h % 2) + 3, :].rearrange("p a n -> p (a n)")[:, 0:P_COLS]
                act.activation(probs[:, h % 8, :], src, ACT.Exp, scale=SCALE).then_inc(S["exp_done"], 1)

            def tanh(b, a):
                act.wait_ge(S["up_done"], b * HCH + a + 1)
                if a >= 2:
                    act.wait_ge(S["hid_l"], b * HCH + a - 1)
                act.activation(gate[:, a % 2, :], bank(2 * (a % 2)), ACT.Tanh, scale=0.5).then_inc(S["tanh_done"], 1)

            def hid_high(b, a):
                act.wait_ge(S["hidden"], b * HCH + a + 1)
                if a >= 2:
                    act.wait_ge(S["down_done"], b * HCH + a - 1)
                act.activation(hid_s[:, a % 2, 0, :], gate[:, a % 2, :], ACT.Copy).then_inc(S["hid_h"], 1)

            def feed_forward(b, ahead):
                for a in range(HCH):
                    tanh(b, a)
                    if ahead and a < TILES:
                        qk_high(b + 1, a)
                    hid_high(b, a)

            act.wait_ge(S["w_qkv_in"], 16)
            act.activation(wqkv_s[:, 0, :, :].rearrange("p c n -> p (c n)"), raw_wqkv, ACT.Copy).then_inc(S["split_h"], 1)
            normalize(0, "x", lambda t: xa[:, t, :], xa, "norm_x")
            xt_high(0)
            for t in range(TILES):
                qk_high(0, t)
            act.wait_ge(S["w_in"], 64)
            for w, raw in ((wo_s, raw_wo), (w1_s, raw_w1), (w3_s, raw_w3)):
                act.activation(w[:, 0, :, :].rearrange("p c n -> p (c n)"), raw, ACT.Copy).then_inc(S["split_h"], 1)
            act.wait_ge(S["const_in"], 16 * 7)
            act.wait_ge(S["zeroed"], 2)
            act.activation(k_t[QK_ROWS:P, :, :], sel[QK_ROWS:P, :].unsqueeze(2).broadcast_to([MAX_ROWS, HEADS, TOKENS]),
                           ACT.Copy).then_inc(S["made_sel"], 1)
            act.wait_ge(S["had_done"], 1)
            act.activation(raw_w2, ps[:, 0:4, :].rearrange("p a n -> p (a n)"), ACT.Copy).then_inc(S["had_copy"], 1)
            act.wait_ge(S["butterfly"], 3)
            act.activation(w2_s[:, 0, :, :].rearrange("p c n -> p (c n)"), stage_a, ACT.Copy, scale=W2_SCALE)\
               .then_inc(S["split_h"], 1)

            def iteration(b, ahead):
                for h in range(HEADS):
                    exps(b, h)
                    if ahead and h == 7:
                        normalize(b + 1, "x", lambda t: xa[:, t, :], xa, "norm_x")
                if ahead:
                    xt_high(b + 1)
                for t in range(TILES):
                    high(b, t, "turned_n", ps[:, 4 + t % 2, 0:DIM].rearrange("p (c n) -> p c n", c=CH),
                         xt2[:, 0, :, t * P:t * P + P], "on_h")
                normalize(b, "y", lambda t: y[:, t, :], y, "norm_y")
                normalize(b, "h", lambda t: xr[:, t, :], y, "norm_h")
                for t in range(TILES):
                    high(b, t, "turned_h", ps[:, 4 + t % 2, 0:DIM].rearrange("p (c n) -> p c n", c=CH),
                         xt2[:, 0, :, t * P:t * P + P], "xt2_h")
                feed_forward(b, ahead)
                normalize(b, "z", lambda t: ps[:, 4 + t // 2, (t % 2) * DIM:(t % 2) * DIM + DIM], y, "norm_z")

            act.sem_inc(S["norm_z"], TILES)
            with act.Fori(0, BATCHES - 1) as b:
                iteration(b, True)
            iteration(BATCHES - 1, False)

        @block.gpsimd
        def _(pool):
            def rope_products(b):
                for t in range(TILES):
                    pool.wait_ge(S["qk_biased"], b * TILES + t + 1)
                    if t >= 2:
                        pool.wait_ge(S["turned_qk"], b * TILES + t - 1)
                    src = qk_b[:, t % 2, :].rearrange("p (h e i) -> p h e i", e=2, i=HALF)
                    shape = [P, 2 * HEADS, 2, HALF]
                    tab = rope_t[:, t, :, :].rearrange("p a (e i) -> p a e i", e=2)
                    pool.tensor_tensor(rot[:, t % 2, :].rearrange("p (h e i) -> p h e i", e=2, i=HALF), src,
                                       tab[:, 0, :, :].unsqueeze(1).broadcast_to(shape), ALU.mult)\
                        .then_inc(S["roped_c"], 1)
                    if t >= 1:
                        pool.wait_ge(S["rotated"], b * TILES + t)
                    o = rot_s.rearrange("p (h e i) -> p h e i", e=2, i=HALF)
                    for e in range(2):
                        ins = pool.tensor_tensor(o[:, :, e, :], src[:, :, 1 - e, :],
                                                 tab[:, 1, e, :].unsqueeze(1).broadcast_to([P, 2 * HEADS, HALF]), ALU.mult)
                    ins.then_inc(S["roped_s"], 1)

            def hid_low(b):
                for a in range(HCH):
                    pool.wait_ge(S["hid_h"], b * HCH + a + 1)
                    pool.tensor_tensor(hid_s[:, a % 2, 1, :], gate[:, a % 2, :], hid_s[:, a % 2, 0, :].bitcast(F32),
                                       ALU.subtract).then_inc(S["hid_l"], 1)

            def cut(b):
                for g in range(GROUPS):
                    pool.wait_ge(S["exp_done"], b * HEADS + 4 * g + 4)
                    pool.sem_inc(S["cutting"], 1)
                    heads = probs[:, 4 * (g % 2):4 * (g % 2) + 4, :]
                    for kt in range(TILES):
                        v = heads[:, :, KEY_COL[kt]:KEY_COL[kt] + P]
                        ins = pool.affine_select(out=v, in_=v, compare_op=ALU.is_ge, fill=0.0, base=0,
                                                 pattern=[[0, 4], [1, P]], channel_multiplier=-1)
                    ins.then_inc(S["masked"], 1)

            pool.memset(k_t[:, 0:HEADS // 2, :].bitcast(F32), 0.0).then_inc(S["zeroed"], 1)
            rope_products(0)
            pool.wait_ge(S["w_in"], 64)
            for n, (w, raw) in enumerate(((wo_s, raw_wo), (w1_s, raw_w1), (w3_s, raw_w3))):
                pool.wait_ge(S["split_h"], n + 2)
                pool.tensor_tensor(w[:, 1, :, :].rearrange("p c n -> p (c n)"), raw,
                                   w[:, 0, :, :].rearrange("p c n -> p (c n)").bitcast(F32), ALU.subtract)\
                    .then_inc(S["split_l"], 1)
            pool.wait_ge(S["split_l"], 4)
            pool.wait_ge(S["had_copy"], 1)
            for n, (src, dst) in enumerate(((raw_w2, stage_a), (stage_a, raw_w2), (raw_w2, stage_a))):
                s4 = src.rearrange("p (a e c) -> p a e c", e=2, c=DIM << n)
                d4 = dst.rearrange("p (a e c) -> p a e c", e=2, c=DIM << n)
                if n:
                    pool.wait_ge(S["butterfly"], n)
                pool.tensor_tensor(d4[:, :, 0, :], s4[:, :, 0, :], s4[:, :, 1, :], ALU.add)
                pool.tensor_tensor(d4[:, :, 1, :], s4[:, :, 0, :], s4[:, :, 1, :], ALU.subtract)\
                    .then_inc(S["butterfly"], 1)
            def iteration(b, ahead):
                cut(b)
                if ahead:
                    rope_products(b + 1)
                hid_low(b)

            with pool.Fori(0, BATCHES - 1) as b:
                iteration(b, True)
            iteration(BATCHES - 1, False)

        @block.vector
        def _(dve):
            def layer_stats(b, which, src):
                done, k = S["ln_" + which], [0]

                def link(ins, last=True):
                    k[0] += 1
                    ins.then_inc(done, 1)
                    if last:
                        dve.wait_ge(done, b * LN_STEPS + k[0])

                for t in range(TILES):
                    link(dve.bn_stats(stats[:, t, :], src(t)), t == TILES - 1)
                total, apart, var, i, a, h = (nw[:, n, :] for n in range(6))
                r, s = rstd[which][:, :], shift[which][:, :]
                link(dve.tensor_tensor(apart, stats[:, :, 1], stats[:, :, 4], ALU.subtract), False)
                link(dve.tensor_tensor(total, stats[:, :, 1], stats[:, :, 4], ALU.add), False)
                link(dve.tensor_tensor(var, stats[:, :, 2], stats[:, :, 5], ALU.add))
                link(dve.scalar_tensor_tensor(out=a, in0=apart, scalar=0.25, in1=apart, op0=ALU.mult, op1=ALU.mult), False)
                link(dve.tensor_scalar(h, var, 1.0 / DIM, EPS, ALU.mult, ALU.add))
                link(dve.tensor_tensor(var, h, a, ALU.add))
                link(dve.tensor_scalar(i.bitcast(I32), var.bitcast(I32), 1, None, ALU.logical_shift_right))
                link(dve.tensor_scalar(r.bitcast(I32), i.bitcast(I32), -1, 0x5F3759DF, ALU.mult, ALU.add))
                for _ in range(NEWTON):
                    link(dve.tensor_tensor(a, r, r, ALU.mult))
                    link(dve.scalar_tensor_tensor(out=h, in0=a, scalar=-0.5, in1=var, op0=ALU.mult, op1=ALU.mult))
                    link(dve.scalar_tensor_tensor(out=r, in0=h, scalar=1.5, in1=r, op0=ALU.add, op1=ALU.mult))
                link(dve.scalar_tensor_tensor(out=s, in0=total, scalar=-0.5, in1=r, op0=ALU.mult, op1=ALU.mult))
                assert k[0] == LN_STEPS

            def low(b, t, ready, src, h, dst, done):
                dve.wait_ge(S[ready], b * TILES + t + 1)
                dve.tensor_tensor(dst, src, h.bitcast(F32), ALU.subtract).then_inc(S[done], 1)

            def xt_low(b):
                for t in range(TILES):
                    c = slice(t * P, t * P + P)
                    low(b, t, "xt_h", ps[:, t % 2, 0:DIM].rearrange("p (c n) -> p c n", c=CH),
                        xt[:, 0, :, c], xt[:, 1, :, c], "xt_l")

            def qk_low(b, t):
                c = slice(t * P, t * P + P)
                low(b, t, "qk_h", ps[:, 6 + t % 2, :].rearrange("p (c n) -> p c n", c=4),
                    qk_s[:, 0, :, c], qk_s[:, 1, :, c], "qk_l")

            def add_bias(b, t):
                dve.wait_ge(S["qkv_done"], b * TILES + t + 1)
                if t >= 2:
                    dve.wait_ge(S["roped_s"], b * TILES + t - 1)
                dve.tensor_tensor(qk_b[:, t % 2, :], bank(t % 2), bqkv[:, 0:2 * DIM], ALU.add)\
                   .then_inc(S["qk_biased"], 1)
                dve.tensor_tensor(v_t[:, t, :, 0:HEAD], ps[:, 2 + t % 2, 0:DIM].rearrange("p (h d) -> p h d", h=HEADS),
                                  bqkv[:, 2 * DIM:3 * DIM].rearrange("p (h d) -> p h d", h=HEADS), ALU.add)\
                   .then_inc(S["v_biased"], 1)

            def rotate(b, t):
                dve.wait_ge(S["roped_s"], b * TILES + t + 1)
                dve.tensor_tensor(rot[:, t % 2, :], rot[:, t % 2, :], rot_s, ALU.add).then_inc(S["rotated"], 1)

            def score_unit(b, n):
                kind, qt, heads = UNITS[n]
                dve.wait_ge(S["scored"], b * N_UNITS + n + 1)
                if kind == "turn":
                    if qt == 0:
                        dve.wait_ge(S["maxrow_in"], b * 16 * PAIRS)
                    dve.tensor_copy(max_row[QK_ROWS:P, qt * P:qt * P + P], ps[0:MAX_ROWS, 6 + n % 2, 0:P])\
                       .then_inc(S["maxed"], 1)
                    return
                keys = (qt + 1) * P
                src = ps[:, 6 + n % 2, 0:keys * len(heads)].rearrange("p (h n) -> p h n", h=len(heads))
                dve.tensor_reduce(maxima[:, heads[0]:heads[0] + len(heads)], src, AX.X, ALU.max).then_inc(S["maxed"], 1)
                if heads[-1] == HEADS - 1:
                    dve.wait_ge(S["maxed"], b * N_UNITS + n + 1)
                    if qt:
                        turn = UNITS.index(("turn", qt - 1, []))
                        dve.wait_ge(S["scored"], b * N_UNITS + turn + 1)
                    dve.tensor_copy(max_s[:, 0, :], maxima[:, :]).then_inc(S["max_h"], 1)
                    dve.wait_ge(S["max_h"], b * TILES + qt + 1)
                    dve.tensor_tensor(max_s[:, 1, :], maxima[:, :], max_s[:, 0, :].bitcast(F32), ALU.subtract)\
                       .then_inc(S["max_l"], 1)
                    dve.wait_ge(S["max_l"], b * TILES + qt + 1)

            def copy_o(b, g):
                dve.wait_ge(S["pv_done"], b * GROUPS + g + 1)
                dve.tensor_copy(o_t[:, g, :], bank(6 + g % 2)).then_inc(S["o_copied"], 1)

            def project(b):
                dve.wait_ge(S["xr_in"], (b + 1) * 16)
                for t in range(TILES + 2):
                    if t < TILES:
                        dve.wait_ge(S["turned_o"], b * TILES + t + 1)
                        src = ps[:, 2 + t % 2, :].rearrange("p (h d) -> p h d", h=HEADS)
                        dve.reciprocal(recip[:, t % 2, :], src[:, :, HEAD]).then_inc(S["recips"], 1)
                        dve.wait_ge(S["recips"], b * TILES + t + 1)
                        dve.tensor_tensor(y[:, t, :].rearrange("p (h d) -> p h d", h=HEADS), src[:, :, 0:HEAD],
                                          recip[:, t % 2, :].unsqueeze(2).broadcast_to([P, HEADS, HEAD]), ALU.mult)\
                           .then_inc(S["normed"], 1)
                    if 1 <= t <= TILES:
                        n = t - 1
                        c = slice(n * P, n * P + P)
                        low(b, n, "on_h", ps[:, 4 + n % 2, 0:DIM].rearrange("p (c n) -> p c n", c=CH),
                            xt2[:, 0, :, c], xt2[:, 1, :, c], "on_l")
                    if t >= 2:
                        n = t - 2
                        dve.wait_ge(S["y_done"], b * TILES + n + 1)
                        dve.tensor_tensor(y[:, n, :], ps[:, 6 + n % 2, 0:DIM], bout[:, :], ALU.add)\
                           .then_inc(S["y_biased"], 1)

            def gate_unit(b, a):
                dve.wait_ge(S["tanh_done"], b * HCH + a + 1)
                dve.scalar_tensor_tensor(out=gate[:, a % 2, :], in0=gate[:, a % 2, :], scalar=1.0,
                                         in1=bank(2 * (a % 2)), op0=ALU.add, op1=ALU.mult).then_inc(S["gated"], 1)
                dve.wait_ge(S["gated"], b * HCH + a + 1)
                dve.tensor_tensor(gate[:, a % 2, :], gate[:, a % 2, :], bank(2 * (a % 2) + 1), ALU.mult)\
                   .then_inc(S["hidden"], 1)

            def iteration(b, ahead):
                if ahead:
                    dve.wait_ge(S["x_in"], (b + 2) * 16)
                    layer_stats(b + 1, "x", lambda t: xa[:, t, :])
                for g in range(GROUPS):
                    copy_o(b, g)
                if ahead:
                    xt_low(b + 1)
                project(b)
                dve.wait_ge(S["y_biased"], (b + 1) * TILES)
                layer_stats(b, "y", lambda t: y[:, t, :])
                if ahead:
                    add_bias(b + 1, 0)
                    add_bias(b + 1, 1)
                for t in range(TILES):
                    dve.wait_ge(S["norm_y"], b * TILES + t + 1)
                    dve.tensor_tensor(xr[:, t, :], xr[:, t, :], y[:, t, :], ALU.add).then_inc(S["resid"], 1)
                dve.wait_ge(S["resid"], (b + 1) * TILES)
                layer_stats(b, "h", lambda t: xr[:, t, :])
                if ahead:
                    for t in range(TILES):
                        if t >= 2:
                            add_bias(b + 1, t)
                        rotate(b + 1, t) if t < 2 else None
                for t in range(TILES):
                    c = slice(t * P, t * P + P)
                    low(b, t, "xt2_h", ps[:, 4 + t % 2, 0:DIM].rearrange("p (c n) -> p c n", c=CH),
                        xt2[:, 0, :, c], xt2[:, 1, :, c], "xt2_l")
                for a in range(HCH + LAG):
                    if a < HCH:
                        gate_unit(b, a)
                    if ahead:
                        if a < TILES:
                            if a < 2:
                                rotate(b + 1, a + 2)
                            qk_low(b + 1, a)
                        for n in range(SPLIT_AT[a], SPLIT_AT[a + 1]):
                            score_unit(b + 1, n)
                dve.wait_ge(S["down_done"], (b + 1) * HCH)
                layer_stats(b, "z", lambda t: ps[:, 4 + t // 2, (t % 2) * DIM:(t % 2) * DIM + DIM])
                for t in range(TILES):
                    dve.wait_ge(S["norm_z"], b * TILES + TILES + t + 1)
                    dve.tensor_tensor(y[:, t, :], xr[:, t, :], y[:, t, :], ALU.add).then_inc(S["final"], 1)

            dve.memset(k_t[:, HEADS // 2:HEADS, :].bitcast(F32), 0.0).then_inc(S["zeroed"], 1)
            dve.memset(v_t[:, :, :, HEAD:2 * HEAD], 1.0).then_inc(S["ones_made"], 1)
            dve.wait_ge(S["x_in"], 16)
            layer_stats(0, "x", lambda t: xa[:, t, :])
            dve.wait_ge(S["split_h"], 1)
            dve.tensor_tensor(wqkv_s[:, 1, :, :].rearrange("p c n -> p (c n)"), raw_wqkv,
                              wqkv_s[:, 0, :, :].rearrange("p c n -> p (c n)").bitcast(F32), ALU.subtract)\
               .then_inc(S["split_l"], 1)
            xt_low(0)
            dve.wait_ge(S["const_in"], 16 * 7)
            dve.tensor_copy(ident_r[:, :], ident[:, :]).then_inc(S["ident_made"], 1)
            dve.tensor_copy(ident_b[:, :], ident[:, :])
            dve.tensor_copy(mask_b[:, :], mask_f[:, :]).then_inc(S["ident_made"], 1)
            for t in range(TILES):
                add_bias(0, t)
                rotate(0, t)
                if t:
                    qk_low(0, t - 1)
            qk_low(0, TILES - 1)
            for n in range(N_UNITS):
                score_unit(0, n)
            dve.wait_ge(S["split_h"], 5)
            dve.scalar_tensor_tensor(out=w2_s[:, 1, :, :].rearrange("p c n -> p (c n)"), in0=stage_a, scalar=W2_SCALE,
                                     in1=w2_s[:, 0, :, :].rearrange("p c n -> p (c n)").bitcast(F32),
                                     op0=ALU.mult, op1=ALU.subtract).then_inc(S["split_l"], 1)
            with dve.Fori(0, BATCHES - 1) as b:
                iteration(b, True)
            iteration(BATCHES - 1, False)


def kernel(**inputs):
    import numpy as np
    import concourse.bacc as bacc
    from concourse.bass_utils import run_bass_kernel_spmd

    nc = bacc.Bacc("TRN2", target_bir_lowering=False, num_devices=1)
    g = {k.split("L0_")[1]: np.asarray(v) for k, v in inputs.items()}
    order = np.arange(3 * DIM).reshape(3, HEADS, HALF, 2)
    order = np.concatenate([order[:2].transpose(0, 1, 3, 2).reshape(-1), order[2].reshape(-1)])
    theta = np.arange(TOKENS, dtype=np.float32)[:, None] * (
        np.float32(10000.0) ** (-np.arange(HALF, dtype=np.float32) / np.float32(HALF)))[None, :]
    cos, sin = np.cos(theta), np.sin(theta)
    had = np.array([[1.0]], np.float32)
    while had.shape[0] < P:
        had = np.block([[had, had], [had, -had]]).astype(np.float32)
    sel = np.zeros((2, HEADS, HEADS), np.float32)
    sel[:] = -np.eye(HEADS, dtype=np.float32)
    arrays = {
        "x": g["attn_x"].reshape(BATCHES * TOKENS, DIM),
        "w_qkv": g["attn_w_qkv"][order].T,
        "b_qkv": g["attn_b_qkv"][order],
        "w_out": g["attn_w_out"].T,
        "b_out": g["attn_b_out"],
        "w1": g["ffn_W1"].T,
        "w3": g["ffn_W3"].T,
        "w2": g["ffn_W2"].T,
        "rope": np.concatenate([cos, cos, -sin, sin], axis=1).astype(np.float32),
        "hadamard": had,
        "eye": np.eye(P, dtype=np.float32),
        "mask": np.triu(np.full((P, P), -1e30, np.float32), 1),
        "selector": sel.reshape(2 * HEADS, HEADS),
    }
    arrays = {f"in_{k}": np.ascontiguousarray(v) for k, v in arrays.items()}
    args = [nc.dram_tensor(k, a.shape, mybir.dt.from_np(a.dtype), kind="ExternalInput").ap() for k, a in arrays.items()]
    out = nc.dram_tensor("out_0", (BATCHES * TOKENS, DIM), F32, kind="ExternalOutput").ap()
    layer_kernel(nc, *args, out)
    r = run_bass_kernel_spmd(nc, [arrays], core_ids=[0])
    return np.asarray(r.results[0]["out_0"]).reshape(BATCHES, TOKENS, DIM)
```

```python
from contextlib import ExitStack

import concourse.bass as bass
from concourse import mybir

F32 = mybir.dt.float32
F32R = mybir.dt.float32r
BF16 = mybir.dt.bfloat16
ALU = mybir.AluOpType
ACT = mybir.ActivationFunctionType
AX = mybir.AxisListType

BATCHES, TOKENS, DIM, HIDDEN, HEADS = 4, 512, 256, 1024, 16
HEAD = DIM // HEADS
P = 128
TILES = TOKENS // P
CH = DIM // P
HCH = HIDDEN // P
PAIRS = HEADS // 2
GROUPS = HEADS // 4
HALF = HEAD // 2
EPS = 1e-5
X_BANK = [0, 1, 2, 5]
H_BANK = [5, 3, 5, 3]
N_BANK = [5, 7, 5, 7]
Y_BANK = [6, 4]
PV_LAG = 6
SCALE = HEAD ** -0.5
W2_SCALE = HIDDEN ** -0.5
QK_ROWS = 3 * 2 * HEAD
MAX_ROWS = 2 * HEADS
KEY_COL = [0, 512, 1024, 896]
P_COLS = 1280
UNITS = []
for _qt in range(TILES):
    _n = TILES // (_qt + 1)
    UNITS += [("scores", _qt, list(range(h, h + _n))) for h in range(0, HEADS, _n)]
N_SCORES = len(UNITS)
for _qt in range(TILES):
    _last = max(i for i, u in enumerate(UNITS) if u[0] == "scores" and u[1] == _qt)
    UNITS.insert(min(_last + 5, len(UNITS)), ("turn", _qt, []))
N_UNITS = len(UNITS)
SCORE_NO = [sum(u[0] == "scores" for u in UNITS[:n]) for n in range(N_UNITS)]


def unit_banks(early):
    banks = [4 + n % 2 for n in range(min(early, N_UNITS))]
    order = [0, 1, 2, 3, 4, 5]
    banks += [order[n % 6] for n in range(N_UNITS - len(banks))]
    return banks[:-1] + [5]


MIX = """o0 o1 d0 d1 n0 n1 q0 l0 l1 e0 c0 o2 d2 y0 o3 s0 n2 y1 l2 d3 s1 n3 y2 v0 l3 q1 r0 y3 s2 s3 e1 c1 t0
    v1 e2 c2 q2 R0 r1 R1 w0 R2 R3 t1 q3 w1 r2 e3 c3 N0 N1 N2 t2 r3 N3 t3 H0 L0 H1 L1 H2 L2 H3 L3 u0 u1
    u2 u3""".split()
FIRST_MIX = "e0 c0 q0 e1 c1 q1 r0 q2 t0 r1 e2 c2 q3 t1 e3 c3 r2 t2 r3 t3".split()
MIX_LAST = """o0 o1 d0 d1 n0 n1 l0 l1 o2 d2 y0 s0 n2 o3 y1 l2 d3 s1 n3 y2 v0 l3 y3 s2 s3 v1 R0 R1 w0 R2 R3 w1 N0
    N1 N2 N3 H0 L0 H1 L1 H2 L2 H3 L3 u0 u1 u2 u3""".split()


def feed_forward_steps(units_after):
    steps, units = [], iter(range(N_UNITS if units_after else 0))
    early = 0

    def some(n):
        nonlocal early
        for _ in range(n):
            steps.append(("unit", next(units), 0))
            early += 1

    for a in range(HCH + 1):
        ups, downs, gap = units_after[a] if units_after else (0, 0, 0)
        for i in range(4 if 0 < a < HCH else 0):
            steps.append(("up", a, i))
            some((ups * (i + 1)) // 4 - (ups * i) // 4)
        if a == HCH:
            some(gap)
        for i in range(TILES if a else 0):
            steps.append(("down", a - 1, i))
            if i == 0 and a < HCH:
                steps.append(("gate", a, 0))
            some((downs * (i + 1)) // 4 - (downs * i) // 4)
        if a == 0:
            steps.append(("gate", a, 0))
    rest = [("unit", n, 0) for n in units]
    z = [("z", 0, 0), ("z", 0, 1), ("ln_z", 0, 0), ("z", 0, 2), ("z", 0, 3), ("ln_z", 0, 1)]
    for half in range(2):
        z += [(kind, 0, 2 * half + t) for kind in ("norm_z", "final") for t in range(2)]
    return steps + rest + z, early


UNITS_AFTER = [(0, 0, 0), (3, 2, 0), (1, 3, 0), (4, 1, 0), (4, 0, 0), (4, 5, 0), (5, 6, 0), (4, 2, 0), (0, 0, 3)]
STEPS, EARLY_UNITS = feed_forward_steps(UNITS_AFTER)
STEPS_LAST, _ = feed_forward_steps(None)
UNIT_BANKS = unit_banks(EARLY_UNITS)
FIRST_UNIT_BANKS = [4 + n % 4 for n in range(N_UNITS - 1)] + [5]
PROBS = 10
FIRST_SELECTOR = [None, 0, 2, 9]
FIRST_TRANSFORM = [-1, -1, -1, -1, -1, 4, 8, 13]
FIRST_W2_PARTS = [14, 19]
ROOT_AFTER = 5
EARLY_SEND = (False, True)
NORMS = {"x": range(4), "y0": range(2), "y1": range(2, 4), "h0": range(2), "h1": range(2, 4),
         "z0": range(2), "z1": range(2, 4)}
LN_STEPS = {n: len(r) + 6 for n, r in NORMS.items()}


def layer_kernel(nc, x, w_qkv, b_qkv, w_out, b_out, w1, w3, w2, rope, hadamard, eye, mask, selector, out):
    ctx = ExitStack()
    with ctx:
        def sb(name, shape, dt=F32):
            return ctx.enter_context(nc.sbuf_tensor(name, shape, dt))

        def sem(name):
            return ctx.enter_context(nc.semaphore(name))

        wqkv_s = sb("wqkv_s", [P, 2, CH, 3 * DIM], F32R)
        wo_s = sb("wo_s", [P, 2, CH, DIM], F32R)
        w1_s = sb("w1_s", [P, 2, CH, HIDDEN], F32R)
        w3_s = sb("w3_s", [P, 2, CH, HIDDEN], F32R)
        w2_s = sb("w2_s", [P, 2, HCH, DIM], F32R)
        bias_s = sb("bias_s", [P, 4 * DIM], F32R)
        sixty_fourth = sb("sixty_fourth", [P, P], F32R)
        rope_t = sb("rope_t", [P, TILES, 2, 2 * HALF])
        ident = sb("ident", [P, P])
        ident_r = sb("ident_r", [P, P], F32R)
        ident_b = sb("ident_b", [P, P], BF16)
        mask_b = sb("mask_b", [P, P], BF16)
        q_t = sb("q_t", [P, PAIRS, TOKENS], F32R)
        k_t = sb("k_t", [P, HEADS, TOKENS], F32R)
        xt = q_t[:, 0:4, :].rearrange("p (s c) t -> p s c t", s=2)
        v_t = sb("v_t", [P, TILES, HEADS, 2 * HEAD])
        def arena(name, words):
            start = nc.sbuf_base
            sb(name, [P, words])

            def place(tensor, shape, dt=F32, word=0):
                words_used = 1
                for n in shape[1:]:
                    words_used *= n
                assert word + words_used <= words
                return nc.alloc_sbuf_tensor_at(tensor, shape, dt, offset=start + 4 * word)
            return place

        place = arena("attend_arena", PROBS * P_COLS)
        probs = place("probs", [P, PROBS, P_COLS])
        qk_s = place("qk_s", [P, 2, 4, TOKENS], F32R)
        qk_b = place("qk_b", [P, 2, 512], word=4096)
        rot = place("rot", [P, 2, 512], word=5120)
        rot_s = place("rot_s", [P, 512], word=6144)[:, :]
        gate = place("gate", [P, 2, TOKENS], word=6656)
        hid_s = place("hid_s", [P, 2, 2, TOKENS], F32R, word=7680)
        raw_bias = place("raw_bias", [P, 4 * DIM], word=9216)[:, :]
        bias_h = place("bias_h", [P, 4 * DIM], F32R, word=10240)[:, :]
        raw_wqkv = place("raw_wqkv", [P, CH * 3 * DIM], word=6656)[:, :]
        raw_wo = place("raw_wo", [P, CH * DIM], word=8192)[:, :]
        had = place("had", [P, P], word=11264)[:, :]
        had_s = place("had_s", [P, 2, P], F32R, word=11264 + P)
        mask_f = place("mask_f", [P, P], word=11264 + 3 * P)[:, :]
        sel = place("sel", [P, HEADS], word=11264 + 4 * P)[:, :]
        place = arena("turned_arena", 2 * CH * TOKENS)
        xt2 = place("xt2", [P, 2, CH, TOKENS], F32R)
        raw_w1 = place("raw_w1", [P, CH * HIDDEN])[:, :]
        o_t = sb("o_t", [P, GROUPS, TOKENS])
        xa = sb("xa", [P, TILES, DIM])
        xy = sb("xy", [P, 2, TILES, DIM])
        xr, y = xy[:, 0, :, :], xy[:, 1, :, :]
        raw_w2 = o_t[:, :, :].rearrange("p a b -> p (a b)")
        raw_w3 = xy[:, :, :, :].rearrange("p a b c -> p (a b c)")
        maxima = sb("maxima", [P, 2, HEADS])
        max_s = sb("max_s", [P, 2, 2, HEADS], F32R)
        recip = sb("recip", [P, 2, HEADS])
        stats = {n: sb("stats_" + n, [P, len(r), 6]) for n, r in NORMS.items()}
        nw = {n: sb("nw_" + n, [P, 6, len(r)]) for n, r in NORMS.items()}
        minus_half = sb("minus_half", [P, TILES])
        spare = sb("spare", [P, 1])
        rstd = {n: sb("rstd_" + n, [P, TILES]) for n in ("x", "y", "h", "z")}
        shift = {n: sb("shift_" + n, [P, TILES]) for n in ("x", "y", "h", "z")}
        scratch = nc.dram_tensor("qk_scratch", [2, 2 * DIM, TOKENS], F32, kind="Internal").ap()
        q_words, k_words = q_t[:, :, :].bitcast(F32), k_t[:, :, :].bitcast(F32)

        ps = ctx.enter_context(nc.psum_tensor("ps", [P, 8, 512], F32))

        names = """x_in w_qkv_in eye_in selector_in bias_in const_in w2_in w_in xr_in
            scratch_in scratch_in_late qk_in qk_in_late out_sent
            split_h split_l w2_h w2_l made_sel zeroed eyes_made half_made bias_h bias_l had_made
            transformed transformed_h transformed_l ones_made
            var_x var_y0 var_y1 var_h0 var_h1 var_z0 var_z1 ln_x ln_y0 ln_y1 ln_h0 ln_h1 ln_z0 ln_z1
            root_x root_y0 root_y1 root_h0 root_h1 root_z0 root_z1
            norm_x turned_x xt_h xt_l qk_done v_done qk_copied v_copied roped_c roped_s rotated
            turned_qk qk_h qk_l cutting scored maxed max_h max_l max_turned rows_in
            st_done exp_done masked pv_done o_copied
            turned_o recips normed turned_n on_h on_l y_done resid norm_h turned_h xt2_h xt2_l
            up_done silu_done hidden hid_h hid_l down_half down_done norm_z final""".split()
        S = {n: sem("s_" + n) for n in names}
        block = ctx.enter_context(nc.Block())

        def bank(n, cols=512):
            return ps[:, n, 0:cols]

        def triple(eng, o, lhs, rhs, first, last, skip=False):
            for n, (i, j) in enumerate(((0, 0), (0, 1), (1, 0))):
                ins = eng.matmul(o, lhs(i), rhs(j), start=first and n == 0, stop=last and n == 2,
                                 skip_group_check=skip)
            return ins

        @block.sync
        def _(sp):
            def load_x(b):
                xv = x[bass.ds(b * TOKENS, TOKENS), :].rearrange("(t p) d -> p t d", p=P)
                sp.dma_start(xa[:, :, :], xv).then_inc(S["x_in"], 16)

            def load_xr(b):
                xv = x[bass.ds(b * TOKENS, TOKENS), :].rearrange("(t p) d -> p t d", p=P)
                sp.dma_start(xr, xv).then_inc(S["xr_in"], 16)

            def pack_qk(b, early_send):
                def halves(half):
                    return slice(half * TOKENS // 2, (half + 1) * TOKENS // 2)

                def send(half):
                    for s, done in ((0, "qk_h"), (1, "qk_l")):
                        sp.wait_ge(S[done], b * TILES + (half + 1) * TILES // 2)
                        sp.dma_start(scratch[s, :, halves(half)].rearrange("(c p) t -> p c t", p=P),
                                     qk_s[:, s, :, halves(half)].bitcast(F32))\
                          .then_inc(S["scratch_in" if half == 0 else "scratch_in_late"], 16)

                def fetch_k(half):
                    c = halves(half)
                    sp.wait_ge(S["scratch_in" if half == 0 else "scratch_in_late"], b * 32 + 32)
                    for j, ks in enumerate((0, 1, 0)):
                        kp = scratch[ks, DIM:2 * DIM, c].rearrange("(a e p) t -> e p a t", e=2, p=HEAD)
                        for e in range(2):
                            dst = k_words[32 * j + HEAD * e:32 * j + HEAD * e + HEAD, :, c]
                            sp.dma_start(dst.rearrange("p (a e) t -> p e a t", e=2)[:, e, :, :], kp[e])\
                              .then_inc(S["qk_in" if half == 0 else "qk_in_late"], 16)

                def fetch_q(half):
                    c = halves(half)
                    for j, qs in enumerate((0, 0, 1)):
                        sp.dma_start(q_words[32 * j:32 * j + 32, :, c],
                                     scratch[qs, 0:DIM, c].rearrange("(a p) t -> p a t", p=32))\
                          .then_inc(S["qk_in" if half == 0 else "qk_in_late"], 16)

                send(0)
                fetch_k(0)
                sp.wait_ge(S["v_done"], b * TILES + TILES)
                if early_send:
                    send(1)
                    fetch_q(0)
                else:
                    fetch_q(0)
                    send(1)
                fetch_k(1)
                fetch_q(1)

            def store(b):
                for half in range(2):
                    tiles = slice(2 * half, 2 * half + 2)
                    sp.wait_ge(S["final"], b * TILES + 2 * half + 2)
                    ov = out[bass.ds(b * TOKENS + half * (TOKENS // 2), TOKENS // 2), :].rearrange("(t p) d -> p t d", p=P)
                    sp.dma_start(ov, y[:, tiles, :]).then_inc(S["out_sent"], 16)

            sp.dma_start(sel[QK_ROWS:P, :], selector).then_inc(S["selector_in"], 16)
            load_x(0)
            sp.dma_start(raw_wqkv.rearrange("p (c n) -> p c n", c=CH),
                         w_qkv.rearrange("(c p) n -> p c n", p=P)).then_inc(S["w_qkv_in"], 16)
            sp.dma_start(ident[:, :], eye).then_inc(S["eye_in"], 16)
            sp.dma_start(raw_bias[:, 0:3 * DIM], b_qkv.partition_broadcast(P)).then_inc(S["bias_in"], 16)
            sp.dma_start(raw_bias[:, 3 * DIM:], b_out.partition_broadcast(P)).then_inc(S["bias_in"], 16)
            sp.dma_start(had, hadamard).then_inc(S["const_in"], 16)
            sp.dma_start(raw_w2.rearrange("p (c n) -> p c n", c=HCH),
                         w2.rearrange("(c p) n -> p c n", p=P)).then_inc(S["w2_in"], 16)
            sp.dma_start(rope_t[:, :, :, :].rearrange("p t a b -> p t (a b)"),
                         rope.rearrange("(t p) a -> p t a", p=P)).then_inc(S["const_in"], 16)
            sp.dma_start(mask_f, mask).then_inc(S["const_in"], 16)
            for w, raw in ((w_out, raw_wo), (w1, raw_w1), (w3, raw_w3)):
                sp.dma_start(raw.rearrange("p (c n) -> p c n", c=CH), w.rearrange("(c p) n -> p c n", p=P))\
                  .then_inc(S["w_in"], 16)
            sp.wait_ge(S["zeroed"], 2)
            pack_qk(0, EARLY_SEND[0])
            load_x(1)
            sp.wait_ge(S["split_l"], 4)
            load_xr(0)
            pack_qk(1, EARLY_SEND[1])
            with sp.Fori(1, BATCHES - 1) as b:
                load_x(b + 1)
                store(b - 1)
                sp.wait_ge(S["out_sent"], b * 32)
                load_xr(b)
                pack_qk(b + 1, EARLY_SEND[1])
            store(BATCHES - 2)
            sp.wait_ge(S["out_sent"], (BATCHES - 1) * 32)
            load_xr(BATCHES - 1)
            store(BATCHES - 1)
            sp.wait_ge(S["out_sent"], 32 * BATCHES)

        @block.tensor
        def _(pe):
            def turn_x(b, t):
                pe.wait_ge(S["norm_x"], b * TILES + t + 1)
                for c in range(CH):
                    ins = pe.transpose(ps[:, X_BANK[t], c * P:c * P + P], xa[:, t, c * P:c * P + P], ident[:, :])
                ins.then_inc(S["turned_x"], 1)

            def qkv(b, t):
                if t == 0:
                    pe.wait_ge(S["xt_l"], b * TILES + TILES)
                else:
                    if t >= 2:
                        pe.wait_ge(S["qk_copied"], b * TILES + t - 1)
                lhs = lambda c: (lambda s: xt[:, s, c, t * P:t * P + P])
                for c in range(CH):
                    triple(pe, ps[:, t % 2, :], lhs(c), lambda s: wqkv_s[:, s, c, 0:2 * DIM], c == 0, False)
                pe.matmul(ps[:, t % 2, :], sixty_fourth[:, :], bias_s[:, 0:2 * DIM], start=False, stop=True)\
                  .then_inc(S["qk_done"], 1)
                if t:
                    pe.wait_ge(S["v_copied"], b * TILES + t)
                for c in range(CH):
                    triple(pe, ps[:, 2, 0:DIM], lhs(c), lambda s: wqkv_s[:, s, c, 2 * DIM:3 * DIM], c == 0, False)
                pe.matmul(ps[:, 2, 0:DIM], sixty_fourth[:, :], bias_s[:, 2 * DIM:3 * DIM], start=False, stop=True)\
                  .then_inc(S["v_done"], 1)

            def turn_qk(b, t):
                pe.wait_ge(S["rotated"], b * TILES + t + 1)
                if t >= 1:
                    pe.wait_ge(S["qk_l"], b * TILES + t)
                for c in range(4):
                    ins = pe.transpose(ps[:, 7, c * P:c * P + P], rot[:, t % 2, c * P:c * P + P], ident[:, :])
                ins.then_inc(S["turned_qk"], 1)

            def score_unit(b, n, banks):
                kind, qt, heads = UNITS[n]
                before = [i for i in range(n) if banks[i] == banks[n]]
                if n == 0:
                    pe.wait_ge(S["qk_in"], (b + 1) * 144)
                    pe.wait_ge(S["qk_l"], b * TILES + TILES)
                if kind == "scores" and qt == TILES // 2 and heads[0] == 0:
                    pe.wait_ge(S["qk_in_late"], (b + 1) * 144)
                if before:
                    if UNITS[before[-1]][0] == "turn":
                        pe.wait_ge(S["rows_in"], 2 * (b * TILES + UNITS[before[-1]][1] + 1))
                    else:
                        pe.wait_ge(S["maxed"], b * N_SCORES + SCORE_NO[before[-1]] + 1)
                else:
                    if banks[n] < 4:
                        pe.wait_ge(S["hidden"], b * HCH)
                o = ps[:, banks[n], :]
                if kind == "turn":
                    pe.wait_ge(S["max_l"], b * TILES + qt + 1)
                    pe.transpose(o[0:MAX_ROWS, 0:P].bitcast(F32R), max_s[:, qt % 2, :, :].rearrange("p s h -> p (s h)"),
                                 ident_r[:, :]).then_inc(S["max_turned"], 1)
                    return
                keys = (qt + 1) * P
                for i, h in enumerate(heads):
                    pe.matmul(o[:, i * keys:(i + 1) * keys], q_t[0:QK_ROWS, h // 2, qt * P:qt * P + P],
                              k_t[0:QK_ROWS, h, 0:keys], start=(i == 0), stop=False, skip_group_check=True)
                    ins = pe.matmul(o[:, (i + 1) * keys - P:(i + 1) * keys], ident_b[:, :], mask_b[:, :],
                                    start=False, stop=(i == len(heads) - 1), skip_group_check=True)
                ins.then_inc(S["scored"], 1)

            def score_t(b, h):
                if h >= 2:
                    pe.wait_ge(S["exp_done"], b * HEADS + h - 1)
                for kt in range(TILES):
                    col = 3 * (h % 2) * 512 + KEY_COL[kt]
                    n = TOKENS - kt * P
                    ins = pe.matmul(ps[:, col // 512, col % 512:col % 512 + n], k_t[:, h, kt * P:kt * P + P],
                                    q_t[:, h // 2, kt * P:TOKENS], start=(kt != 3), stop=(kt != 1), skip_group_check=True)
                ins.then_inc(S["st_done"], 1)

            def values(b, g, kt):
                if kt == 0:
                    if g == 0:
                        pe.wait_ge(S["norm_z"], b * TILES + TILES)
                    pe.wait_ge(S["masked"], b * HEADS + 4 * g + 4)
                    if g >= 2:
                        pe.wait_ge(S["o_copied"], b * GROUPS + g - 1)
                for j in range(4):
                    h = 4 * g + j
                    ins = pe.matmul(ps[32 * j:32 * j + 32, 6 + g % 2, kt * P:TOKENS], v_t[:, kt, h, :],
                                    probs[:, h % PROBS, KEY_COL[kt]:KEY_COL[kt] + TOKENS - kt * P],
                                    start=(kt == 0), stop=(kt == TILES - 1), skip_group_check=True)
                if kt == TILES - 1:
                    ins.then_inc(S["pv_done"], 1)

            def attend(b, ahead):
                pe.wait_ge(S["rows_in"], 2 * (b + 1) * TILES - 1)
                pe.wait_ge(S["maxed"], (b + 1) * N_SCORES)
                for h in range(HEADS + PV_LAG):
                    if h == 1:
                        pe.wait_ge(S["rows_in"], 2 * (b + 1) * TILES)
                    if h < HEADS:
                        score_t(b, h)
                    if h == HEADS + 1 and ahead:
                        pe.wait_ge(S["exp_done"], b * HEADS + HEADS)
                        for t in range(TILES):
                            turn_x(b + 1, t)
                    if h >= PV_LAG:
                        values(b, (h - PV_LAG) // 4, (h - PV_LAG) % 4)

            def turn_o(b, t):
                if t == 0:
                    pe.wait_ge(S["o_copied"], b * GROUPS + GROUPS)
                if t >= 2:
                    pe.wait_ge(S["normed"], b * TILES + t - 1)
                for g in range(GROUPS):
                    ins = pe.transpose(ps[:, 3 + t % 2, g * P:g * P + P], o_t[:, g, t * P:t * P + P], ident[:, :])
                ins.then_inc(S["turned_o"], 1)

            def turn_n(b, t):
                pe.wait_ge(S["normed"], b * TILES + t + 1)
                if t >= 2:
                    pe.wait_ge(S["on_l"], b * TILES + t - 1)
                for c in range(CH):
                    ins = pe.transpose(ps[:, N_BANK[t], c * P:c * P + P], y[:, t, c * P:c * P + P], ident[:, :])
                ins.then_inc(S["turned_n"], 1)

            def out_product(b, t):
                pe.wait_ge(S["on_l"], b * TILES + t + 1)
                if t % 2:
                    pe.wait_ge(S["var_y%d" % (t // 2)], b * LN_STEPS["y0"] + 1)
                o = ps[:, Y_BANK[t // 2], (t % 2) * DIM:(t % 2) * DIM + DIM]
                for c in range(CH):
                    triple(pe, o, lambda s: xt2[:, s, c, t * P:t * P + P],
                           lambda s: wo_s[:, s, c, :], c == 0 and t % 2 == 0, False, skip=True)
                pe.matmul(o, sixty_fourth[:, :], bias_s[:, 3 * DIM:4 * DIM], start=False, stop=t % 2 == 1,
                          skip_group_check=True).then_inc(S["y_done"], 1)

            def turn_h(b, t):
                pe.wait_ge(S["norm_h"], b * TILES + t + 1)
                if t >= 2:
                    pe.wait_ge(S["xt2_l"], b * TILES + t - 1)
                for c in range(CH):
                    ins = pe.transpose(ps[:, H_BANK[t], c * P:c * P + P], y[:, t, c * P:c * P + P], ident[:, :])
                ins.then_inc(S["turned_h"], 1)

            def mix(b, order):
                for m in order:
                    t = int(m[1]) if m[1:].isdigit() else 0
                    if m[0] == "q":
                        qkv(b + 1, t)
                    elif m[0] == "r":
                        turn_qk(b + 1, t)
                    elif m[0] == "o":
                        turn_o(b, t)
                    elif m[0] == "n":
                        turn_n(b, t)
                    elif m[0] == "y":
                        out_product(b, t)
                    elif m[0] == "H":
                        turn_h(b, t)
                    elif m[0] == "u":
                        up(b, 0, t)

            def up(b, a, i):
                half, n = i // 2, i % 2
                if a == 0 and n == 0:
                    pe.wait_ge(S["xt2_l"], b * TILES + 2 * half + 2)
                if a >= 2 and i == 0:
                    pe.wait_ge(S["hidden"], b * HCH + a - 1)
                w, c = (w1_s, w3_s)[n], slice(half * TOKENS // 2, (half + 1) * TOKENS // 2)
                for k in range(CH):
                    ins = triple(pe, ps[:, 2 * (a % 2) + n, c], lambda s: w[:, s, k, a * P:a * P + P],
                                 lambda s: xt2[:, s, k, c], k == 0 and half == 0, k == CH - 1 and half == 1, skip=True)
                if i == 3:
                    ins.then_inc(S["up_done"], 1)

            def down(b, a, t):
                if t == 0:
                    pe.wait_ge(S["hid_l"], b * HCH + a + 1)
                ins = triple(pe, ps[:, 6 + t // 2, (t % 2) * DIM:(t % 2) * DIM + DIM],
                             lambda s: hid_s[:, a % 2, s, t * P:t * P + P], lambda s: w2_s[:, s, a, :],
                             a == 0 and t % 2 == 0, a == HCH - 1 and t % 2 == 1, skip=True)
                if a == HCH - 1 and t == TILES // 2 - 1:
                    ins.then_inc(S["down_half"], 1)
                if t == TILES - 1:
                    ins.then_inc(S["down_done"], 1)

            def feed_forward(b, steps):
                for kind, n, i in steps:
                    if kind == "up":
                        up(b, n, i)
                    elif kind == "down":
                        down(b, n, i)
                    elif kind == "unit":
                        score_unit(b + 1, n, UNIT_BANKS)

            def transform(c):
                for i in range(HCH):
                    sign = bin(i & c).count("1") % 2
                    for s in range(2):
                        ins = pe.matmul(ps[:, c // 2, (c % 2) * DIM:(c % 2) * DIM + DIM], had_s[:, sign, :],
                                        w2_s[:, s, i, :], start=(c % 2 == 0 and i == 0 and s == 0),
                                        stop=(c % 2 == 1 and i == HCH - 1 and s == 1), skip_group_check=True)
                ins.then_inc(S["transformed"], 1)

            pe.wait_ge(S["eye_in"], 16)
            for t in range(TILES):
                turn_x(0, t)
            pe.wait_ge(S["split_l"], 1)
            pe.wait_ge(S["bias_h"], 2)
            pe.wait_ge(S["bias_l"], 1)
            mix(-1, FIRST_MIX)
            pe.wait_ge(S["had_made"], 2)
            pe.wait_ge(S["w2_l"], 1)
            pe.wait_ge(S["v_copied"], TILES)
            for c in range(HCH):
                if FIRST_TRANSFORM[c] < 0:
                    transform(c)
            pe.wait_ge(S["eyes_made"], 3)
            for n in range(N_UNITS):
                score_unit(0, n, FIRST_UNIT_BANKS)
                for c in range(HCH):
                    if FIRST_TRANSFORM[c] == n:
                        transform(c)
            pe.wait_ge(S["made_sel"], 4)
            pe.wait_ge(S["ones_made"], 1)
            pe.wait_ge(S["split_l"], 4)
            pe.wait_ge(S["transformed_l"], 1)
            with pe.Fori(0, BATCHES - 1) as b:
                attend(b, True)
                mix(b, MIX)
                feed_forward(b, STEPS)
            attend(BATCHES - 1, False)
            mix(BATCHES - 1, MIX_LAST)
            feed_forward(BATCHES - 1, STEPS_LAST)

        @block.scalar
        def _(act):
            def high(b, t, turned, src, dst, done):
                act.wait_ge(S[turned], b * TILES + t + 1)
                act.activation(dst, src, ACT.Copy).then_inc(S[done], 1)

            def two(src):
                return src.rearrange("p (c n) -> p c n", n=P)

            def xt_high(b, t):
                high(b, t, "turned_x", two(ps[:, X_BANK[t], 0:DIM]), xt[:, 0, :, t * P:t * P + P], "xt_h")

            def qk_high(b, t):
                high(b, t, "turned_qk", two(ps[:, 7, :]), qk_s[:, 0, :, t * P:t * P + P], "qk_h")

            def copy_qkv(b, t):
                act.wait_ge(S["qk_done"], b * TILES + t + 1)
                if t >= 2:
                    act.wait_ge(S["roped_s"], b * TILES + t - 1)
                    act.wait_ge(S["roped_c"], b * TILES + t - 1)
                act.activation(qk_b[:, t % 2, :], bank(t % 2), ACT.Copy).then_inc(S["qk_copied"], 1)
                act.wait_ge(S["v_done"], b * TILES + t + 1)
                act.activation(v_t[:, t, :, 0:HEAD], ps[:, 2, 0:DIM].rearrange("p (h d) -> p h d", h=HEADS), ACT.Copy)\
                   .then_inc(S["v_copied"], 1)

            def exps(b, h):
                if h >= PROBS:
                    act.wait_ge(S["pv_done"], b * GROUPS + (h - PROBS) // 4 + 1)
                act.wait_ge(S["st_done"], b * HEADS + h + 1)
                src = ps[:, 3 * (h % 2):3 * (h % 2) + 3, :].rearrange("p a n -> p (a n)")[:, 0:P_COLS]
                act.activation(probs[:, h % PROBS, :], src, ACT.Exp, scale=SCALE).then_inc(S["exp_done"], 1)

            def silu(b, a):
                act.wait_ge(S["up_done"], b * HCH + a + 1)
                if a >= 2:
                    act.wait_ge(S["hid_l"], b * HCH + a - 1)
                act.activation(gate[:, a % 2, :], bank(2 * (a % 2)), ACT.Silu).then_inc(S["silu_done"], 1)

            def hid_high(b, a):
                act.wait_ge(S["hidden"], b * HCH + a + 1)
                if a >= 2:
                    act.wait_ge(S["down_done"], b * HCH + a - 1)
                act.activation(hid_s[:, a % 2, 0, :], gate[:, a % 2, :], ACT.Copy).then_inc(S["hid_h"], 1)

            def score_unit(b, n, banks):
                kind, qt, heads = UNITS[n]
                if kind == "turn":
                    act.wait_ge(S["max_turned"], b * TILES + qt + 1)
                    for first, pairs in ((0, 1), (1, PAIRS - 1)):
                        act.activation(q_t[QK_ROWS:P, first:first + pairs, qt * P:qt * P + P],
                                       ps[0:MAX_ROWS, banks[n], 0:P].unsqueeze(1).broadcast_to([MAX_ROWS, pairs, P]),
                                       ACT.Copy).then_inc(S["rows_in"], 1)
                elif heads[-1] == HEADS - 1:
                    act.wait_ge(S["maxed"], b * N_SCORES + SCORE_NO[n] + 1)
                    if qt >= 2:
                        act.wait_ge(S["max_turned"], b * TILES + qt - 1)
                    act.activation(max_s[:, qt % 2, 0, :], maxima[:, qt % 2, :], ACT.Copy).then_inc(S["max_h"], 1)

            def mix(b, order):
                for m in order:
                    t = int(m[1]) if m[1:].isdigit() else 0
                    if m[0] == "q":
                        copy_qkv(b + 1, t)
                    elif m[0] == "r":
                        qk_high(b + 1, t)
                    elif m[0] == "n":
                        high(b, t, "turned_n", two(ps[:, N_BANK[t], 0:DIM]), xt2[:, 0, :, t * P:t * P + P], "on_h")
                    elif m == "N0":
                        act.activation(spare[:, :], minus_half[:, 0:1], ACT.Silu)
                    elif m[0] == "H":
                        high(b, t, "turned_h", two(ps[:, H_BANK[t], 0:DIM]), xt2[:, 0, :, t * P:t * P + P], "xt2_h")
                    elif m == "u3":
                        silu(b, 0)

            def feed_forward(b, steps):
                for kind, n, i in steps:
                    if kind == "up" and i == 3:
                        silu(b, n)
                    elif kind == "gate":
                        hid_high(b, n)
                        if n == HCH - 1:
                            act.activation(spare[:, :], minus_half[:, 0:1], ACT.Exp)
                    elif kind == "unit":
                        score_unit(b + 1, n, UNIT_BANKS)

            def split(w, raw):
                act.activation(w[:, 0, :, :].rearrange("p c n -> p (c n)"), raw, ACT.Copy).then_inc(S["split_h"], 1)

            def select(n):
                h = slice(4 * n, 4 * n + 4)
                act.activation(k_t[QK_ROWS:P, h, :], sel[QK_ROWS:P, h].unsqueeze(2).broadcast_to([MAX_ROWS, 4, TOKENS]),
                               ACT.Copy).then_inc(S["made_sel"], 1)

            act.wait_ge(S["selector_in"], 16)
            select(0)
            act.wait_ge(S["w_qkv_in"], 16)
            split(wqkv_s, raw_wqkv)
            act.wait_ge(S["bias_in"], 32)
            act.activation(bias_h, raw_bias, ACT.Copy).then_inc(S["bias_h"], 1)
            act.activation(bias_s[0:P // 2, :], raw_bias[0:P // 2, :], ACT.Copy)
            act.wait_ge(S["eye_in"], 16)
            act.activation(sixty_fourth[:, :], ident[:, :], ACT.Identity, scale=0.0, bias=2.0 / P).then_inc(S["bias_h"], 1)
            for t in range(TILES):
                xt_high(0, t)
            act.wait_ge(S["w2_in"], 16)
            act.activation(w2_s[:, 0, :, :].rearrange("p c n -> p (c n)"), raw_w2, ACT.Copy).then_inc(S["w2_h"], 1)
            mix(-1, FIRST_MIX)
            act.wait_ge(S["w_in"], 48)
            split(w1_s, raw_w1)
            split(wo_s, raw_wo)
            split(w3_s, raw_w3)
            for n in range(N_UNITS):
                score_unit(0, n, FIRST_UNIT_BANKS)
                if n in FIRST_SELECTOR:
                    select(FIRST_SELECTOR.index(n))
                if n == FIRST_W2_PARTS[0]:
                    act.wait_ge(S["transformed"], HCH)
                    act.activation(w2_s[:, 0, :, :].rearrange("p c n -> p (c n)"),
                                   ps[:, 0:4, :].rearrange("p a n -> p (a n)"), ACT.Copy, scale=W2_SCALE)\
                       .then_inc(S["transformed_h"], 1)

            def iteration(b, order, steps):
                for h in range(HEADS):
                    exps(b, h)
                if order is MIX:
                    for t in range(TILES):
                        xt_high(b + 1, t)
                mix(b, order)
                feed_forward(b, steps)

            act.sem_inc(S["norm_z"], TILES)
            with act.Fori(0, BATCHES - 1) as b:
                iteration(b, MIX, STEPS)
            iteration(BATCHES - 1, MIX_LAST, STEPS_LAST)

        @block.gpsimd
        def _(pool):
            def root(b, which):
                tiles = slice(NORMS[which][0], NORMS[which][-1] + 1)
                r, s = rstd[which[0]][:, tiles], shift[which[0]][:, tiles]
                pool.wait_ge(S["var_" + which], (b + 1) * LN_STEPS[which])
                pool.tensor_tensor(r, nw[which][:, 5, :], minus_half[:, tiles], ALU.pow)\
                    .then_inc(S["root_" + which], 1)
                pool.wait_ge(S["root_" + which], b + 1)
                pool.tensor_tensor(s, nw[which][:, 4, :], r, ALU.mult)\
                    .then_inc(S["ln_" + which], 1)
                if which[0] == "z":
                    pool.wait_ge(S["ln_" + which], 2 * b + 1)
                    pool.tensor_tensor(s, s, shift["y"][:, tiles], ALU.add).then_inc(S["ln_" + which], 1)

            def rope_products(b, t):
                pool.wait_ge(S["qk_copied"], b * TILES + t + 1)
                src = qk_b[:, t % 2, :].rearrange("p (h e i) -> p h e i", e=2, i=HALF)
                tab = rope_t[:, t, :, :].rearrange("p a (e i) -> p a e i", e=2)
                if t >= 1:
                    pool.wait_ge(S["rotated"], b * TILES + t)
                o = rot_s.rearrange("p (h e i) -> p h e i", e=2, i=HALF)
                for e in range(2):
                    ins = pool.tensor_tensor(o[:, :, e, :], src[:, :, 1 - e, :],
                                             tab[:, 1, e, :].unsqueeze(1).broadcast_to([P, 2 * HEADS, HALF]), ALU.mult)
                ins.then_inc(S["roped_s"], 1)

            def hid_low(b, a):
                pool.wait_ge(S["hid_h"], b * HCH + a + 1)
                pool.tensor_tensor(hid_s[:, a % 2, 1, :], gate[:, a % 2, :], hid_s[:, a % 2, 0, :].bitcast(F32),
                                   ALU.subtract).then_inc(S["hid_l"], 1)

            def max_low(b, n):
                kind, qt, heads = UNITS[n]
                if kind == "scores" and heads[-1] == HEADS - 1:
                    pool.wait_ge(S["max_h"], b * TILES + qt + 1)
                    pool.tensor_tensor(max_s[:, qt % 2, 1, :], maxima[:, qt % 2, :], max_s[:, qt % 2, 0, :].bitcast(F32),
                                       ALU.subtract).then_inc(S["max_l"], 1)

            def cut(b, h):
                pool.wait_ge(S["exp_done"], b * HEADS + h + 1)
                pool.sem_inc(S["cutting"], 1)
                head = probs[:, h % PROBS, :]
                v = bass.AP(tensor=head.tensor, offset=head.offset, ap=[head.ap[0], [512, 3], [1, P]])
                pool.affine_select(out=v, in_=v, compare_op=ALU.is_ge, fill=0.0, base=0,
                                   pattern=[[0, 3], [1, P]], channel_multiplier=-1)
                v = head[:, KEY_COL[3]:KEY_COL[3] + P]
                pool.affine_select(out=v, in_=v, compare_op=ALU.is_ge, fill=0.0, base=0,
                                   pattern=[[1, P]], channel_multiplier=-1).then_inc(S["masked"], 1)

            def iteration(b, order, steps):
                for h in range(HEADS):
                    cut(b, h)
                    if h == ROOT_AFTER and order is MIX:
                        root(b + 1, "x")
                for m in order:
                    if m[0] == "e":
                        rope_products(b + 1, int(m[1]))
                    elif m[0] in "vw":
                        root(b, {"v": "y", "w": "h"}[m[0]] + m[1])
                for kind, n, i in steps:
                    if kind == "gate":
                        hid_low(b, n)
                    elif kind == "unit":
                        max_low(b + 1, n)
                    elif kind == "ln_z":
                        root(b, "z%d" % i)

            pool.memset(minus_half[:, :], -0.5).then_inc(S["half_made"], 1)
            pool.wait_ge(S["half_made"], 1)
            pool.memset(k_t[0:QK_ROWS, 0:HEADS // 2, :].bitcast(F32), 0.0).then_inc(S["zeroed"], 1)
            root(0, "x")
            pool.wait_ge(S["const_in"], 48)
            for m in FIRST_MIX:
                if m[0] == "e":
                    rope_products(0, int(m[1]))
            for n, (w, raw) in enumerate(((wo_s, raw_wo), (w3_s, raw_w3))):
                pool.wait_ge(S["split_h"], n + 3)
                pool.tensor_tensor(w[:, 1, :, :].rearrange("p c n -> p (c n)"), raw,
                                   w[:, 0, :, :].rearrange("p c n -> p (c n)").bitcast(F32), ALU.subtract)\
                    .then_inc(S["split_l"], 1)
            for n in range(N_UNITS):
                max_low(0, n)
            with pool.Fori(0, BATCHES - 1) as b:
                iteration(b, MIX, STEPS)
            iteration(BATCHES - 1, MIX_LAST, STEPS_LAST)

        @block.vector
        def _(dve):
            def tile_stats(which, t, src):
                dve.bn_stats(stats[which][:, t - NORMS[which][0], :], src).then_inc(S["var_" + which], 1)

            def variance(b, which):
                done, tiles, steps = S["var_" + which], len(NORMS[which]), LN_STEPS[which]
                k = [tiles]

                def link(ins, last=True):
                    k[0] += 1
                    ins.then_inc(done, 1)
                    if last:
                        dve.wait_ge(done, b * steps + k[0])

                dve.wait_ge(done, b * steps + tiles)
                st = stats[which]
                total, apart, squares, spread, negative, var = (nw[which][:, n, :] for n in range(6))
                link(dve.tensor_tensor(apart, st[:, :, 1], st[:, :, 4], ALU.subtract), False)
                link(dve.scalar_tensor_tensor(out=squares, in0=st[:, :, 2], scalar=DIM * EPS, in1=st[:, :, 5],
                                              op0=ALU.add, op1=ALU.add), False)
                link(dve.tensor_tensor(total, st[:, :, 1], st[:, :, 4], ALU.add))
                link(dve.tensor_scalar(negative, total, -0.5, None, ALU.mult), False)
                link(dve.scalar_tensor_tensor(out=spread, in0=apart, scalar=0.25, in1=apart, op0=ALU.mult, op1=ALU.mult))
                link(dve.scalar_tensor_tensor(out=var, in0=squares, scalar=1.0 / DIM, in1=spread, op0=ALU.mult, op1=ALU.add), False)
                assert k[0] == steps

            def low(b, t, ready, src, h, dst, done):
                dve.wait_ge(S[ready], b * TILES + t + 1)
                dve.tensor_tensor(dst, src, h.bitcast(F32), ALU.subtract).then_inc(S[done], 1)

            def two(src):
                return src.rearrange("p (c n) -> p c n", n=P)

            def xt_low(b, t):
                c = slice(t * P, t * P + P)
                low(b, t, "xt_h", two(ps[:, X_BANK[t], 0:DIM]), xt[:, 0, :, c], xt[:, 1, :, c], "xt_l")

            def qk_low(b, t):
                c = slice(t * P, t * P + P)
                low(b, t, "qk_h", two(ps[:, 7, :]), qk_s[:, 0, :, c], qk_s[:, 1, :, c], "qk_l")

            def rope_cos(b, t):
                dve.wait_ge(S["qk_copied"], b * TILES + t + 1)
                if t >= 2:
                    dve.wait_ge(S["turned_qk"], b * TILES + t - 1)
                dve.tensor_tensor(rot[:, t % 2, :].rearrange("p (h e) -> p h e", e=HEAD),
                                  qk_b[:, t % 2, :].rearrange("p (h e) -> p h e", e=HEAD),
                                  rope_t[:, t, 0, :].unsqueeze(1).broadcast_to([P, 2 * HEADS, HEAD]), ALU.mult)\
                   .then_inc(S["roped_c"], 1)

            def rotate(b, t):
                dve.wait_ge(S["roped_s"], b * TILES + t + 1)
                dve.wait_ge(S["roped_c"], b * TILES + t + 1)
                dve.tensor_tensor(rot[:, t % 2, :], rot[:, t % 2, :], rot_s, ALU.add).then_inc(S["rotated"], 1)

            def score_unit(b, n, banks):
                kind, qt, heads = UNITS[n]
                if kind == "turn":
                    return
                dve.wait_ge(S["scored"], b * N_SCORES + SCORE_NO[n] + 1)
                if qt >= 2 and heads[0] == 0:
                    dve.wait_ge(S["max_l"], b * TILES + qt - 1)
                keys = (qt + 1) * P
                src = ps[:, banks[n], 0:keys * len(heads)].rearrange("p (h n) -> p h n", h=len(heads))
                dve.tensor_reduce(maxima[:, qt % 2, heads[0]:heads[0] + len(heads)], src, AX.X, ALU.max)\
                   .then_inc(S["maxed"], 1)

            def copy_o(b, g):
                dve.wait_ge(S["pv_done"], b * GROUPS + g + 1)
                dve.tensor_copy(o_t[:, g, :], bank(6 + g % 2)).then_inc(S["o_copied"], 1)

            def norm_x(b):
                dve.wait_ge(S["ln_x"], b + 1)
                for t in range(TILES):
                    dve.tensor_scalar(xa[:, t, :], xa[:, t, :], rstd["x"][:, t:t + 1], shift["x"][:, t:t + 1],
                                      ALU.mult, ALU.add).then_inc(S["norm_x"], 1)

            def sums(b, t):
                if t == 0:
                    dve.wait_ge(S["xr_in"], (b + 1) * 16)
                dve.wait_ge(S["turned_o"], b * TILES + t + 1)
                src = ps[:, 3 + t % 2, :].rearrange("p (h d) -> p h d", h=HEADS)
                dve.reciprocal(recip[:, t % 2, :], src[:, :, HEAD]).then_inc(S["recips"], 1)

            def quotient(b, t):
                dve.wait_ge(S["recips"], b * TILES + t + 1)
                src = ps[:, 3 + t % 2, :].rearrange("p (h d) -> p h d", h=HEADS)
                dve.tensor_tensor(y[:, t, :].rearrange("p (h d) -> p h d", h=HEADS), src[:, :, 0:HEAD],
                                  recip[:, t % 2, :].unsqueeze(2).broadcast_to([P, HEADS, HEAD]), ALU.mult)\
                   .then_inc(S["normed"], 1)

            def projected(t):
                return ps[:, Y_BANK[t // 2], (t % 2) * DIM:(t % 2) * DIM + DIM]

            def mix(b, order):
                for m in order:
                    t = int(m[1]) if m[1:].isdigit() else 0
                    c = slice(t * P, t * P + P)
                    if m[0] == "c":
                        rope_cos(b + 1, t)
                    elif m[0] == "r":
                        rotate(b + 1, t)
                    elif m[0] == "t":
                        qk_low(b + 1, t)
                    elif m[0] == "o":
                        sums(b, t)
                    elif m[0] == "d":
                        quotient(b, t)
                    elif m[0] == "v":
                        variance(b, "y" + m[1])
                    elif m[0] == "w":
                        dve.wait_ge(S["resid"], b * TILES + 2 * t + 2)
                        tile_stats("h" + m[1], 2 * t + 1, xr[:, 2 * t + 1, :])
                        variance(b, "h" + m[1])
                    elif m[0] == "l":
                        low(b, t, "on_h", two(ps[:, N_BANK[t], 0:DIM]), xt2[:, 0, :, c], xt2[:, 1, :, c], "on_l")
                    elif m[0] == "s":
                        dve.wait_ge(S["y_done"], b * TILES + t + 1)
                        tile_stats("y%d" % (t // 2), t, projected(t))
                    elif m[0] == "R":
                        dve.wait_ge(S["ln_y%d" % (t // 2)], b + 1)
                        dve.scalar_tensor_tensor(out=xr[:, t, :], in0=projected(t), scalar=rstd["y"][:, t:t + 1],
                                                 in1=xr[:, t, :], op0=ALU.mult, op1=ALU.add).then_inc(S["resid"], 1)
                        if t % 2:
                            dve.wait_ge(S["resid"], b * TILES + t)
                            tile_stats("h%d" % (t // 2), t - 1, xr[:, t - 1, :])
                    elif m[0] == "N":
                        dve.wait_ge(S["ln_h%d" % (t // 2)], b + 1)
                        dve.tensor_scalar(y[:, t, :], xr[:, t, :], rstd["h"][:, t:t + 1], shift["h"][:, t:t + 1],
                                          ALU.mult, ALU.add).then_inc(S["norm_h"], 1)
                    elif m[0] == "L":
                        low(b, t, "xt2_h", two(ps[:, H_BANK[t], 0:DIM]), xt2[:, 0, :, c], xt2[:, 1, :, c], "xt2_l")

            def feed_forward(b, steps):
                for kind, n, i in steps:
                    if kind == "gate":
                        dve.wait_ge(S["silu_done"], b * HCH + n + 1)
                        dve.tensor_tensor(gate[:, n % 2, :], gate[:, n % 2, :], bank(2 * (n % 2) + 1), ALU.mult)\
                           .then_inc(S["hidden"], 1)
                    elif kind == "unit":
                        score_unit(b + 1, n, UNIT_BANKS)
                    elif kind == "z":
                        if i < TILES // 2:
                            dve.wait_ge(S["down_half"], b + 1)
                        else:
                            dve.wait_ge(S["down_done"], (b + 1) * HCH)
                        tile_stats("z%d" % (i // 2), i, ps[:, 6 + i // 2, (i % 2) * DIM:(i % 2) * DIM + DIM])
                    elif kind == "ln_z":
                        variance(b, "z%d" % i)
                    elif kind == "norm_z":
                        dve.wait_ge(S["ln_z%d" % (i // 2)], 2 * b + 2)
                        dve.scalar_tensor_tensor(out=y[:, i, :], in0=ps[:, 6 + i // 2, (i % 2) * DIM:(i % 2) * DIM + DIM],
                                                 scalar=rstd["z"][:, i:i + 1], in1=xr[:, i, :],
                                                 op0=ALU.mult, op1=ALU.add).then_inc(S["norm_z"], 1)
                    elif kind == "final":
                        dve.wait_ge(S["norm_z"], b * TILES + TILES + i + 1)
                        dve.tensor_scalar(y[:, i, :], y[:, i, :], shift["z"][:, i:i + 1], None, ALU.add)\
                           .then_inc(S["final"], 1)

            def layer_x(b):
                dve.wait_ge(S["x_in"], (b + 1) * 16)
                for t in range(TILES):
                    tile_stats("x", t, xa[:, t, :])
                variance(b, "x")

            def iteration(b, order, steps):
                if order is MIX:
                    layer_x(b + 1)
                copy_o(b, 0)
                if order is MIX:
                    norm_x(b + 1)
                copy_o(b, 1)
                copy_o(b, 2)
                if order is MIX:
                    for t in range(TILES):
                        xt_low(b + 1, t)
                copy_o(b, 3)
                mix(b, order)
                feed_forward(b, steps)

            def split(w, raw, n):
                dve.wait_ge(S["split_h"], n)
                dve.tensor_tensor(w[:, 1, :, :].rearrange("p c n -> p (c n)"), raw,
                                  w[:, 0, :, :].rearrange("p c n -> p (c n)").bitcast(F32), ALU.subtract)\
                   .then_inc(S["split_l"], 1)

            dve.memset(k_t[0:QK_ROWS, HEADS // 2:HEADS, :].bitcast(F32), 0.0).then_inc(S["zeroed"], 1)
            dve.memset(v_t[:, :, :, HEAD:2 * HEAD], 1.0).then_inc(S["ones_made"], 1)
            layer_x(0)
            split(wqkv_s, raw_wqkv, 1)
            norm_x(0)
            dve.wait_ge(S["bias_h"], 1)
            for t in range(TILES):
                xt_low(0, t)
            dve.tensor_tensor(bias_s[P // 2:P, :], raw_bias[P // 2:P, :], bias_h[P // 2:P, :].bitcast(F32), ALU.subtract)\
               .then_inc(S["bias_l"], 1)
            dve.wait_ge(S["const_in"], 48)
            dve.tensor_copy(had_s[:, 0, :], had).then_inc(S["had_made"], 1)
            dve.tensor_scalar(had_s[:, 1, :], had, -1.0, None, ALU.mult).then_inc(S["had_made"], 1)
            dve.wait_ge(S["w2_h"], 1)
            dve.tensor_tensor(w2_s[:, 1, :, :].rearrange("p c n -> p (c n)"), raw_w2,
                              w2_s[:, 0, :, :].rearrange("p c n -> p (c n)").bitcast(F32), ALU.subtract)\
               .then_inc(S["w2_l"], 1)
            mix(-1, FIRST_MIX)
            dve.tensor_copy(ident_r[:, :], ident[:, :]).then_inc(S["eyes_made"], 1)
            dve.tensor_copy(ident_b[:, :], ident[:, :]).then_inc(S["eyes_made"], 1)
            dve.tensor_copy(mask_b[:, :], mask_f).then_inc(S["eyes_made"], 1)
            split(w1_s, raw_w1, 2)
            for n in range(N_UNITS):
                score_unit(0, n, FIRST_UNIT_BANKS)
                if n == FIRST_W2_PARTS[1]:
                    dve.wait_ge(S["transformed_h"], 1)
                    dve.scalar_tensor_tensor(out=w2_s[:, 1, :, :].rearrange("p c n -> p (c n)"),
                                             in0=ps[:, 0:4, :].rearrange("p a n -> p (a n)"), scalar=W2_SCALE,
                                             in1=w2_s[:, 0, :, :].rearrange("p c n -> p (c n)").bitcast(F32),
                                             op0=ALU.mult, op1=ALU.subtract).then_inc(S["transformed_l"], 1)
            with dve.Fori(0, BATCHES - 1) as b:
                iteration(b, MIX, STEPS)
            iteration(BATCHES - 1, MIX_LAST, STEPS_LAST)


def kernel(**inputs):
    import numpy as np
    import concourse.bacc as bacc
    from concourse.bass_utils import run_bass_kernel_spmd

    nc = bacc.Bacc("TRN2", target_bir_lowering=False, num_devices=1)
    g = {k.split("L0_")[1]: np.asarray(v) for k, v in inputs.items()}
    order = np.arange(3 * DIM).reshape(3, HEADS, HALF, 2)
    order = np.concatenate([order[:2].transpose(0, 1, 3, 2).reshape(-1), order[2].reshape(-1)])
    theta = np.arange(TOKENS, dtype=np.float32)[:, None] * (
        np.float32(10000.0) ** (-np.arange(HALF, dtype=np.float32) / np.float32(HALF)))[None, :]
    cos, sin = np.cos(theta), np.sin(theta)
    had = np.array([[1.0]], np.float32)
    while had.shape[0] < P:
        had = np.block([[had, had], [had, -had]]).astype(np.float32)
    sel = np.zeros((2, HEADS, HEADS), np.float32)
    sel[:] = -np.eye(HEADS, dtype=np.float32)
    arrays = {
        "x": g["attn_x"].reshape(BATCHES * TOKENS, DIM),
        "w_qkv": g["attn_w_qkv"][order].T,
        "b_qkv": g["attn_b_qkv"][order],
        "w_out": g["attn_w_out"].T,
        "b_out": g["attn_b_out"],
        "w1": g["ffn_W1"].T,
        "w3": g["ffn_W3"].T,
        "w2": g["ffn_W2"].T,
        "rope": np.concatenate([cos, cos, -sin, sin], axis=1).astype(np.float32),
        "hadamard": had,
        "eye": np.eye(P, dtype=np.float32),
        "mask": np.triu(np.full((P, P), -1e30, np.float32), 1),
        "selector": sel.reshape(2 * HEADS, HEADS),
    }
    arrays = {f"in_{k}": np.ascontiguousarray(v) for k, v in arrays.items()}
    args = [nc.dram_tensor(k, a.shape, mybir.dt.from_np(a.dtype), kind="ExternalInput").ap() for k, a in arrays.items()]
    out = nc.dram_tensor("out_0", (BATCHES * TOKENS, DIM), F32, kind="ExternalOutput").ap()
    layer_kernel(nc, *args, out)
    r = run_bass_kernel_spmd(nc, [arrays], core_ids=[0])
    return np.asarray(r.results[0]["out_0"]).reshape(BATCHES, TOKENS, DIM)
```
